# Optimizing a Trainium2 kernel written in Bass

```python
import numpy as np
import jax
import jax.numpy as jnp

def _softmax(x, axis=-1):
    return jax.nn.softmax(x, axis=axis)

def _gelu(x):
    return jax.nn.gelu(x, approximate=True)

def _silu(x):
    return jax.nn.silu(x)

def _sigmoid(x):
    return jax.nn.sigmoid(x)

def _layernorm(x, axis=-1, eps=1e-05):
    m = jnp.mean(x, axis=axis, keepdims=True)
    v = jnp.var(x, axis=axis, keepdims=True)
    return (x - m) / jnp.sqrt(v + eps)

def _scatter_add(tgt, idx, src, axis=0):
    return tgt.at[idx].add(src)

def _segment_sum(src, seg, n):
    return jax.ops.segment_sum(src, seg, n)
kernel_name = 'mk_pixart_resid_d1_seqx_r8_0818f0'

def setup_inputs(seed: int=0):
    np.random.seed(seed)
    _w = jnp.asarray

    def _rec_inputs():
        import jax
        import jax.numpy as jnp
        _rk = jax.random.key(seed)
        x = -0.0002928 + 1 * jax.random.normal(jax.random.fold_in(_rk, 1), (2, 512, 128), jnp.float32)
        _lenS = 512 - jax.random.randint(jax.random.fold_in(_rk, 7), (2,), 0, max(1, 512 // 4) + 1, jnp.int32)
        _lenS2 = 32 - jax.random.randint(jax.random.fold_in(_rk, 8), (2,), 0, max(1, 32 // 4) + 1, jnp.int32)
        cond_1024 = 0.000887014 + 1.03683 * jax.random.normal(jax.random.fold_in(_rk, 11), (2, 128), jnp.float32)
        _ctx_1024P = jax.random.normal(jax.random.fold_in(_rk, 12), (2, 16, 128), jnp.float32)
        _ctx_1024c = jax.random.dirichlet(jax.random.fold_in(_rk, 512), 0.3 * jnp.ones((16,), jnp.float32), (2, 32))
        _ctx_1024t = jnp.einsum('bsk,bkd->bsd', _ctx_1024c, _ctx_1024P)
        _ctx_1024t = _ctx_1024t * jax.lax.rsqrt(jnp.mean(jnp.square(_ctx_1024t)) + 1e-12) * 0.953939
        ctx_1024 = -0.000761806 + 0.999296 * (_ctx_1024t + 0.3 * jax.random.normal(jax.random.fold_in(_rk, 612), (2, 32, 128), jnp.float32))
        return (x, cond_1024, ctx_1024)
    x, cond_1024, ctx_1024 = _rec_inputs()

    def _L0_xcond_setup():
        import jax, jax.numpy as jnp
        import numpy as np
        import math
        B, S, CTX, D, H, DH = (2, 256, 32, 128, 16, 64)
        INNER = H * DH
        DFF = 4 * D

        def layernorm(x, eps=1e-05):
            m = jnp.mean(x, axis=-1, keepdims=True)
            v = jnp.var(x, axis=-1, keepdims=True)
            return (x - m) * jax.lax.rsqrt(v + eps)

        def adaln(x, t, w, b):
            emb = t @ w + b
            scale, shift = jnp.split(emb, 2, axis=-1)
            return layernorm(x) * (1.0 + scale) + shift

        def mha(xq, ctx, wq, wk, wv, wo, bo):
            b, sq, _ = xq.shape
            sk = ctx.shape[1]
            q = (xq @ wq).reshape(b, sq, H, DH).transpose(0, 2, 1, 3)
            k = (ctx @ wk).reshape(b, sk, H, DH).transpose(0, 2, 1, 3)
            v = (ctx @ wv).reshape(b, sk, H, DH).transpose(0, 2, 1, 3)
            scores = jnp.einsum('bhqd,bhkd->bhqk', q, k) / math.sqrt(DH)
            attn = jax.nn.softmax(scores, axis=-1)
            out = jnp.einsum('bhqk,bhkd->bhqd', attn, v)
            out = out.transpose(0, 2, 1, 3).reshape(b, sq, INNER)
            return out @ wo + bo

        def glu_ff(x, w1, b1, w2, b2):
            u = x @ w1 + b1
            a, gate = jnp.split(u, 2, axis=-1)
            return a * jax.nn.gelu(gate, approximate=False) @ w2 + b2
        key = jax.random.key(seed)
        ks = jax.random.split(key, 24)
        s = 1.0 / math.sqrt(D)

        def n(k, shape, scale=1.0):
            return jax.random.normal(k, shape, dtype=jnp.float32) * scale
        return {'x': n(ks[0], (B, S, D)), 't': n(ks[1], (B, 1, D)), 'context': n(ks[2], (B, CTX, D)), 'attn1_wq': n(ks[3], (D, INNER), s), 'attn1_wk': n(ks[4], (D, INNER), s), 'attn1_wv': n(ks[5], (D, INNER), s), 'attn1_wo': n(ks[6], (INNER, D), s), 'attn1_bo': n(ks[7], (D,), 0.01), 'attn2_wq': n(ks[8], (D, INNER), s), 'attn2_wk': n(ks[9], (D, INNER), s), 'attn2_wv': n(ks[10], (D, INNER), s), 'attn2_wo': n(ks[11], (INNER, D), s), 'attn2_bo': n(ks[12], (D,), 0.01), 'ff_w1': n(ks[13], (D, 2 * DFF), s), 'ff_b1': n(ks[14], (2 * DFF,), 0.01), 'ff_w2': n(ks[15], (DFF, D), 1.0 / math.sqrt(DFF)), 'ff_b2': n(ks[16], (D,), 0.01), 'norm1_w': n(ks[17], (D, 2 * D), s), 'norm1_b': n(ks[18], (2 * D,), 0.01), 'norm2_w': n(ks[19], (D, 2 * D), s), 'norm2_b': n(ks[20], (2 * D,), 0.01), 'norm3_w': n(ks[21], (D, 2 * D), s), 'norm3_b': n(ks[22], (2 * D,), 0.01)}
    _L0_xcond_all = _L0_xcond_setup()
    _L0_xcond_in = {k: v for k, v in _L0_xcond_all.items() if k in ('attn1_wq', 'attn1_wk', 'attn1_wv', 'attn1_wo', 'attn1_bo', 'attn2_wq', 'attn2_wk', 'attn2_wv', 'attn2_wo', 'attn2_bo', 'ff_w1', 'ff_b1', 'ff_w2', 'ff_b2', 'norm1_w', 'norm1_b', 'norm2_w', 'norm2_b', 'norm3_w', 'norm3_b')}
    del _L0_xcond_all

    def _L0_ffn_setup():
        import jax, jax.numpy as jnp
        import numpy as np
        B, S, D, F, E = (2, 256, 128, 512, 8)
        LN_EPS = 1e-05

        def _xavier(key, shape, fan_in, fan_out):
            a = np.sqrt(6.0 / (fan_in + fan_out))
            return jax.random.uniform(key, shape, jnp.float32, -a, a)
        key = jax.random.key(seed)
        ks = jax.random.split(key, 8)
        tgt = jax.random.normal(ks[0], (B, S, D), jnp.float32)
        router_w = _xavier(ks[1], (E, D), D, E)
        router_b = jnp.zeros((E,), jnp.float32)
        w1 = _xavier(ks[2], (E, D, F), D, F)
        b1 = jnp.zeros((E, F), jnp.float32)
        w2 = _xavier(ks[3], (E, F, D), F, D)
        b2 = jnp.zeros((E, D), jnp.float32)
        gamma = jnp.ones((D,), jnp.float32)
        beta = jnp.zeros((D,), jnp.float32)
        return {'tgt': tgt, 'router_w': router_w, 'router_b': router_b, 'w1': w1, 'b1': b1, 'w2': w2, 'b2': b2, 'gamma': gamma, 'beta': beta}
    _L0_ffn_all = _L0_ffn_setup()
    _L0_ffn_in = {k: v for k, v in _L0_ffn_all.items() if k in ('router_w', 'router_b', 'w1', 'b1', 'w2', 'b2', 'gamma', 'beta')}
    del _L0_ffn_all
    return {'x': x, 'cond_1024': cond_1024, 'ctx_1024': ctx_1024, 'L0_xcond_attn1_wq': _L0_xcond_in['attn1_wq'], 'L0_xcond_attn1_wk': _L0_xcond_in['attn1_wk'], 'L0_xcond_attn1_wv': _L0_xcond_in['attn1_wv'], 'L0_xcond_attn1_wo': _L0_xcond_in['attn1_wo'], 'L0_xcond_attn1_bo': _L0_xcond_in['attn1_bo'], 'L0_xcond_attn2_wq': _L0_xcond_in['attn2_wq'], 'L0_xcond_attn2_wk': _L0_xcond_in['attn2_wk'], 'L0_xcond_attn2_wv': _L0_xcond_in['attn2_wv'], 'L0_xcond_attn2_wo': _L0_xcond_in['attn2_wo'], 'L0_xcond_attn2_bo': _L0_xcond_in['attn2_bo'], 'L0_xcond_ff_w1': _L0_xcond_in['ff_w1'], 'L0_xcond_ff_b1': _L0_xcond_in['ff_b1'], 'L0_xcond_ff_w2': _L0_xcond_in['ff_w2'], 'L0_xcond_ff_b2': _L0_xcond_in['ff_b2'], 'L0_xcond_norm1_w': _L0_xcond_in['norm1_w'], 'L0_xcond_norm1_b': _L0_xcond_in['norm1_b'], 'L0_xcond_norm2_w': _L0_xcond_in['norm2_w'], 'L0_xcond_norm2_b': _L0_xcond_in['norm2_b'], 'L0_xcond_norm3_w': _L0_xcond_in['norm3_w'], 'L0_xcond_norm3_b': _L0_xcond_in['norm3_b'], 'L0_ffn_router_w': _L0_ffn_in['router_w'], 'L0_ffn_router_b': _L0_ffn_in['router_b'], 'L0_ffn_w1': _L0_ffn_in['w1'], 'L0_ffn_b1': _L0_ffn_in['b1'], 'L0_ffn_w2': _L0_ffn_in['w2'], 'L0_ffn_b2': _L0_ffn_in['b2'], 'L0_ffn_gamma': _L0_ffn_in['gamma'], 'L0_ffn_beta': _L0_ffn_in['beta']}

def reference(x, cond_1024, ctx_1024, L0_xcond_attn1_wq, L0_xcond_attn1_wk, L0_xcond_attn1_wv, L0_xcond_attn1_wo, L0_xcond_attn1_bo, L0_xcond_attn2_wq, L0_xcond_attn2_wk, L0_xcond_attn2_wv, L0_xcond_attn2_wo, L0_xcond_attn2_bo, L0_xcond_ff_w1, L0_xcond_ff_b1, L0_xcond_ff_w2, L0_xcond_ff_b2, L0_xcond_norm1_w, L0_xcond_norm1_b, L0_xcond_norm2_w, L0_xcond_norm2_b, L0_xcond_norm3_w, L0_xcond_norm3_b, L0_ffn_router_w, L0_ffn_router_b, L0_ffn_w1, L0_ffn_b1, L0_ffn_w2, L0_ffn_b2, L0_ffn_gamma, L0_ffn_beta):
    import jax
    import jax.numpy as jnp

    def _L0_xcond_ref(x, t, context, attn1_wq, attn1_wk, attn1_wv, attn1_wo, attn1_bo, attn2_wq, attn2_wk, attn2_wv, attn2_wo, attn2_bo, ff_w1, ff_b1, ff_w2, ff_b2, norm1_w, norm1_b, norm2_w, norm2_b, norm3_w, norm3_b):
        import jax, jax.numpy as jnp
        import numpy as np
        import math
        B, S, CTX, D, H, DH = (2, 256, 32, 128, 16, 64)
        INNER = H * DH
        DFF = 4 * D

        def layernorm(x, eps=1e-05):
            m = jnp.mean(x, axis=-1, keepdims=True)
            v = jnp.var(x, axis=-1, keepdims=True)
            return (x - m) * jax.lax.rsqrt(v + eps)

        def adaln(x, t, w, b):
            emb = t @ w + b
            scale, shift = jnp.split(emb, 2, axis=-1)
            return layernorm(x) * (1.0 + scale) + shift

        def mha(xq, ctx, wq, wk, wv, wo, bo):
            b, sq, _ = xq.shape
            sk = ctx.shape[1]
            q = (xq @ wq).reshape(b, sq, H, DH).transpose(0, 2, 1, 3)
            k = (ctx @ wk).reshape(b, sk, H, DH).transpose(0, 2, 1, 3)
            v = (ctx @ wv).reshape(b, sk, H, DH).transpose(0, 2, 1, 3)
            scores = jnp.einsum('bhqd,bhkd->bhqk', q, k) / math.sqrt(DH)
            attn = jax.nn.softmax(scores, axis=-1)
            out = jnp.einsum('bhqk,bhkd->bhqd', attn, v)
            out = out.transpose(0, 2, 1, 3).reshape(b, sq, INNER)
            return out @ wo + bo

        def glu_ff(x, w1, b1, w2, b2):
            u = x @ w1 + b1
            a, gate = jnp.split(u, 2, axis=-1)
            return a * jax.nn.gelu(gate, approximate=False) @ w2 + b2
        h1 = adaln(x, t, norm1_w, norm1_b)
        x = mha(h1, h1, attn1_wq, attn1_wk, attn1_wv, attn1_wo, attn1_bo) + x
        h2 = adaln(x, t, norm2_w, norm2_b)
        x = mha(h2, context, attn2_wq, attn2_wk, attn2_wv, attn2_wo, attn2_bo) + x
        h3 = adaln(x, t, norm3_w, norm3_b)
        x = glu_ff(h3, ff_w1, ff_b1, ff_w2, ff_b2) + x
        return x

    def _L0_ffn_ref(tgt, router_w, router_b, w1, b1, w2, b2, gamma, beta):
        import jax, jax.numpy as jnp
        import numpy as np
        B, S, D, F, E = (2, 256, 128, 512, 8)
        LN_EPS = 1e-05

        def _xavier(key, shape, fan_in, fan_out):
            a = np.sqrt(6.0 / (fan_in + fan_out))
            return jax.random.uniform(key, shape, jnp.float32, -a, a)
        logits = jnp.einsum('bsd,ed->bse', tgt, router_w) + router_b
        rw = jax.nn.softmax(logits, axis=-1)
        rw = jnp.zeros_like(rw).at[..., 0].set(1.0)
        h = jax.nn.relu(jnp.einsum('bsd,edf->besf', tgt, w1) + b1[None, :, None, :])
        eo = jnp.einsum('besf,efd->besd', h, w2) + b2[None, :, None, :]
        tgt2 = jnp.einsum('besd,bse->bsd', eo, rw)
        x = tgt + tgt2
        mean = jnp.mean(x, axis=-1, keepdims=True)
        var = jnp.mean(jnp.square(x - mean), axis=-1, keepdims=True)
        return (x - mean) * jax.lax.rsqrt(var + LN_EPS) * gamma + beta
    x = x + _L0_xcond_ref(_layernorm(x, axis=-1), cond_1024[:, None, :], ctx_1024, L0_xcond_attn1_wq, L0_xcond_attn1_wk, L0_xcond_attn1_wv, L0_xcond_attn1_wo, L0_xcond_attn1_bo, L0_xcond_attn2_wq, L0_xcond_attn2_wk, L0_xcond_attn2_wv, L0_xcond_attn2_wo, L0_xcond_attn2_bo, L0_xcond_ff_w1, L0_xcond_ff_b1, L0_xcond_ff_w2, L0_xcond_ff_b2, L0_xcond_norm1_w, L0_xcond_norm1_b, L0_xcond_norm2_w, L0_xcond_norm2_b, L0_xcond_norm3_w, L0_xcond_norm3_b)
    x = x + _L0_ffn_ref(_layernorm(x, axis=-1), L0_ffn_router_w, L0_ffn_router_b, L0_ffn_w1, L0_ffn_b1, L0_ffn_w2, L0_ffn_b2, L0_ffn_gamma, L0_ffn_beta)
    return x

_drawn_inputs = setup_inputs


def setup_inputs(seed=0):
    import zlib

    import numpy as np

    out = dict(_drawn_inputs(seed))
    spreads = {'L0_ffn_router_b': (0.0, 0.1),
     'L0_ffn_b1': (0.0, 0.581),
     'L0_ffn_b2': (0.0, 0.531),
     'L0_ffn_gamma': (1.0, 0.2),
     'L0_ffn_beta': (0.0, 0.443)}
    factors = {'L0_xcond_attn1_bo': 22.047,
     'L0_xcond_attn2_bo': 25.421,
     'L0_xcond_ff_b1': 8.0,
     'L0_xcond_ff_b2': 27.707,
     'L0_xcond_norm1_b': 5.836,
     'L0_xcond_norm2_b': 8.0,
     'L0_xcond_norm3_b': 8.0}
    for name, (base, spread) in spreads.items():
        noise = np.random.default_rng([zlib.crc32(name.encode()), seed]).standard_normal(out[name].shape)
        drawn = base * np.exp(spread * noise) if base else spread * noise
        out[name] = jnp.asarray(drawn.astype(out[name].dtype))
    for name, factor in factors.items():
        out[name] = (out[name] * factor).astype(out[name].dtype)
    return out
```

```python
from contextlib import ExitStack

import concourse.bass as bass
from concourse import mybir

F32 = mybir.dt.float32
ALU = mybir.AluOpType
ACT = mybir.ActivationFunctionType
AX_X = mybir.AxisListType.X
ds = bass.ds

P = 128
B, S, D, H, DH, CTX = 2, 512, 128, 16, 64, 32
QT = S // P
NT = B * QT
PAIRS = H // 2
STEPS = B * QT
DFF = 4 * D
FFC = DFF // P
SCALE = 1.0 / 8.0
EPS = 1e-5
NLN = 6

R_COND, R_N1, R_N2, R_N3, R_FB1, R_EB1 = 0, 2, 4, 6, 8, 16
ROWS = 20
V_FB2, V_BO2, V_EB2, V_GAMMA, V_BETA = range(5)


def residual_block(nc, a, out):
    x_d = a["x"].rearrange("b (t p) d -> p (b t) d", p=P)
    out_d = out.rearrange("b (t p) d -> p (b t) d", p=P)
    pre = "L0_xcond_"
    wq_d, wk_d, wv_d = (a[pre + f"attn1_w{c}"] for c in "qkv")
    wo_d = a[pre + "attn1_wo"].rearrange("(c p) d -> p c d", p=P)
    wo2_d = a[pre + "attn2_wo"].rearrange("(c p) d -> p c d", p=P)
    fw2_d = a[pre + "ff_w2"].rearrange("(c p) d -> p c d", p=P)
    ew1_d = a["L0_ffn_w1"][0]
    ew2_d = a["L0_ffn_w2"][0].rearrange("(c p) d -> p c d", p=P)

    with ExitStack() as ctx:
        def sb(name, *shape):
            return ctx.enter_context(nc.sbuf_tensor(name, list(shape), F32))

        def sem(name):
            return ctx.enter_context(nc.semaphore(name))

        x = sb("x", P, NT, D)
        xn = sb("xn", P, NT, D)
        r1 = sb("r1", P, NT, D)
        r1b = sb("r1b", P, NT, D)
        r2 = sb("r2", P, NT, D)
        r2b = sb("r2b", P, NT, D)
        r3 = sb("r3", P, NT, D)
        tgt = sb("tgt", P, NT, D)
        tgtb = sb("tgtb", P, NT, D)
        z = sb("z", P, NT, D)
        zn = sb("zn", P, NT, D)
        n = sb("n", P, NT, D)
        res = sb("res", P, NT, D)
        stats = sb("stats", P, NT, 6)
        meanvar = sb("meanvar", P, NLN, NT, 2)
        rstd = sb("rstd", P, NLN, NT)
        half = sb("half", P, QT)
        ident = sb("ident", P, P)
        ones = sb("ones", 1, P)
        rows = sb("rows", ROWS, P)
        cols = sb("cols", P, ROWS)
        spread = sb("spread", P, 5, D)
        bo1row = sb("bo1row", 1, QT, D)
        nw = sb("nw", P, 3, 2 * D)
        mod = sb("mod", P, 3, 2, B)
        h1T = sb("h1T", P, B, S)
        h2T = sb("h2T", P, B, S)
        h3T = sb("h3T", P, B, S)
        tT = sb("tT", P, B, S)
        stage = sb("stage", P, 2, P)
        wv = sb("wv", P, H * DH)
        wo = sb("wo", P, PAIRS, D)
        wqT = sb("wqT", P, P)
        wkT = sb("wkT", P, 2, P)
        M = sb("M", P, 2, P)
        G = sb("G", P, B, 2, S)
        V = sb("V", P, B, QT, 2 * DH)
        prob = sb("prob", P, 2, 2, S)
        negmax = sb("negmax", P, 2, 2)
        psumr = sb("psumr", P, 2, 2)
        rsum = sb("rsum", P, 2, 2)
        PT = sb("PT", P, B, 2, QT, S)
        OT = sb("OT", P, S)
        ctxt = sb("ctxt", B * CTX, D)
        ctxT = sb("ctxT", P, B * CTX)
        wq2 = sb("wq2", P, H * DH)
        wk2 = sb("wk2", P, H * DH)
        wv2 = sb("wv2", P, H * DH)
        wo2 = sb("wo2", P, PAIRS, D)
        wq2T = sb("wq2T", P, PAIRS, P)
        bdK = sb("bdK", P, PAIRS, B, 2, CTX)
        bdV = sb("bdV", P, PAIRS, B, 2, CTX)
        A2 = sb("A2", P, B, PAIRS, 2 * CTX)
        B2 = sb("B2", P, B, 4, D)
        e2 = sb("e2", P, 2, H, CTX)
        m2 = sb("m2", P, 2, H)
        s2 = sb("s2", P, 2, H)
        i2 = sb("i2", P, 2, H)
        PT2 = sb("PT2", P, 2, 4, P)
        fw1 = sb("fw1", P, 2 * DFF)
        fw2 = sb("fw2", P, FFC, D)
        ew1 = sb("ew1", P, DFF)
        ew2 = sb("ew2", P, FFC, D)
        gate = sb("gate", P, 2, S)
        hid = PT[:, :, 0, :, :]
        ehid = PT[:, :, 1, :, :]

        bank = [ctx.enter_context(nc.psum_tensor(f"bank{k}", [P, 512], F32)) for k in range(8)]
        y_ps = bank[0:2]
        s_ps = bank[2:4]
        t_ps = bank[4:6]
        o_ps = bank[6]
        p_ps = bank[7]

        x_in = [sem("x_in0"), sem("x_in1")]
        rows_in, nw_in, spread_in = sem("rows_in"), sem("nw_in"), sem("spread_in")
        stage_in, wv_in, wo_in = sem("stage_in"), sem("wv_in"), sem("wo_in")
        w2_in, ff_in, ew_in = sem("w2_in"), sem("ff_in"), sem("ew_in")
        stored = sem("stored")
        const_set, ident_done, zero_set = sem("const_set"), sem("ident_done"), sem("zero_set")
        cols_ps, cols_set, mod_ps, mod_set = sem("cols_ps"), sem("cols_set"), sem("mod_ps"), sem("mod_set")
        stat_done, aggr_done, eps_done = sem("stat_done"), sem("aggr_done"), sem("eps_done")
        rstd_done, normed = sem("rstd_done"), sem("normed")
        turned, hT_done = sem("turned"), sem("hT_done")
        proj_done, proj_read = sem("proj_done"), sem("proj_read")
        scored, maxed, exped = sem("scored"), sem("maxed"), sem("exped")
        summed, probs_ready = sem("summed"), sem("probs_ready")
        p_turned, p_read = sem("p_turned"), sem("p_read")
        pv_done, o_read, y_added = sem("pv_done"), sem("o_read"), sem("y_added")
        c_ps, c_read = sem("c_ps"), sem("c_read")
        sc2_done, max2_done, sub2_done = sem("sc2_done"), sem("max2_done"), sem("sub2_done")
        exp2_done, sum2_done, inv2_done, nrm2_done = sem("exp2_done"), sem("sum2_done"), sem("inv2_done"), sem("nrm2_done")
        t2_done, t2_read, out2_done = sem("t2_done"), sem("t2_read"), sem("out2_done")
        r1_done, r1b_done, r2_done, r2b_done = sem("r1_done"), sem("r1b_done"), sem("r2_done"), sem("r2b_done")
        r3_done, tgtb_done, z_done, zg_done, zb_done = sem("r3_done"), sem("tgtb_done"), sem("z_done"), sem("zg_done"), sem("zb_done")
        xr_done = sem("xr_done")
        res_done = sem("res_done")
        gate_ps, gate_read, lin_ps, hid_done = sem("gate_ps"), sem("gate_read"), sem("lin_ps"), sem("hid_done")
        ff_ps, eh_ps, eh_done, e_ps = sem("ff_ps"), sem("eh_ps"), sem("eh_done"), sem("e_ps")

        PROJ_BEFORE = 4
        PROJ_ROUND = 8

        def projections(i, last):
            c = i * PROJ_ROUND + PROJ_BEFORE
            ahead = {0: ("G", 1, 0, c), 1: ("G", 1, 1, c + 1), 2: ("W", 0, 0, c + 2), 3: ("V", 0, 0, c + 4),
                     4: ("G", 0, 0, c + 5), 5: ("G", 0, 1, c + 6), 6: ("V", 1, 0, c + 7)}
            behind = {2: ("M", 0, 0, c + 3)}
            if last:
                ahead = {0: ("G", 1, 0, c), 1: ("G", 1, 1, c + 1), 3: ("V", 0, 0, c + 2), 6: ("V", 1, 0, c + 3)}
                behind = {}
            return ahead, behind

        def rounds(eng, body):
            body(0, True, False)
            with eng.Fori(1, PAIRS - 1) as i:
                body(i, False, False)
            body(PAIRS - 1, False, True)

        block = ctx.enter_context(nc.Block())

        @block.sync
        def _(sp):
            for b in range(B):
                sp.dma_start(x[:, b * QT:(b + 1) * QT, :], x_d[:, b * QT:(b + 1) * QT, :]).then_inc(x_in[b], 16)
            sp.dma_start(stage[:, 0, :], wq_d[:, 0:P]).then_inc(stage_in, 16)
            sp.dma_start(stage[:, 1, :], wk_d[:, 0:P]).then_inc(stage_in, 16)
            sp.dma_start(wv[:, :], wv_d).then_inc(wv_in, 16)
            sp.dma_start(wo[:, :, :], wo_d).then_inc(wo_in, 16)

            def next_stage(i):
                sp.wait_ge(proj_done, i * PROJ_ROUND + PROJ_BEFORE + 3 - PROJ_ROUND)
                sp.dma_start(stage[:, 0, :], wq_d[:, ds((i + 1) * P, P)]).then_inc(stage_in, 16)
                sp.dma_start(stage[:, 1, :], wk_d[:, ds((i + 1) * P, P)]).then_inc(stage_in, 16)

            sp.wait_ge(proj_done, 1)
            sp.dma_start(stage[:, 0, :], wq_d[:, P:2 * P]).then_inc(stage_in, 16)
            sp.dma_start(stage[:, 1, :], wk_d[:, P:2 * P]).then_inc(stage_in, 16)
            sp.dma_start(ctxt[:, :], a["ctx_1024"].rearrange("b c d -> (b c) d")).then_inc(w2_in, 16)
            sp.dma_start(wq2[:, :], a[pre + "attn2_wq"]).then_inc(w2_in, 16)
            sp.dma_start(wk2[:, :], a[pre + "attn2_wk"]).then_inc(w2_in, 16)
            sp.dma_start(wv2[:, :], a[pre + "attn2_wv"]).then_inc(w2_in, 16)
            sp.dma_start(wo2[:, :, :], wo2_d).then_inc(w2_in, 16)
            sp.dma_start(fw1[:, :], a[pre + "ff_w1"]).then_inc(ff_in, 16)
            sp.dma_start(fw2[:, :, :], fw2_d).then_inc(ff_in, 16)
            sp.dma_start(ew1[:, :], ew1_d).then_inc(ew_in, 16)
            sp.dma_start(ew2[:, :, :], ew2_d).then_inc(ew_in, 16)
            with sp.Fori(1, PAIRS - 1) as i:
                next_stage(i)

            for b in range(B):
                sp.wait_ge(res_done, b + 1)
                sp.dma_start(out_d[:, b * QT:(b + 1) * QT, :], res[:, b * QT:(b + 1) * QT, :]).then_inc(stored, 16)
            sp.wait_ge(stored, 16 * B)

        @block.gpsimd
        def _(pool):
            nc.gpsimd.memset(ident[:, :], 0.0).then_inc(const_set, 1)
            nc.gpsimd.memset(half[:, :], -0.5).then_inc(const_set, 1)
            nc.gpsimd.memset(ones[:, :], 1.0).then_inc(const_set, 1)
            pool.wait_ge(const_set, 3)
            nc.gpsimd.affine_select(out=ident[:, :], in_=ident[:, :], compare_op=ALU.not_equal, fill=1.0,
                                    base=0, pattern=[[-1, P]], channel_multiplier=1).then_inc(ident_done, 1)
            nc.gpsimd.memset(wkT[:, :, :], 0.0).then_inc(zero_set, 1)

            def power(k, b):
                c = 2 * k + b + 1
                var = meanvar[:, k, b * QT:(b + 1) * QT, 1]
                r = rstd[:, k, b * QT:(b + 1) * QT]
                pool.wait_ge(aggr_done, QT * c)
                nc.gpsimd.tensor_scalar(r, var, EPS, None, ALU.add).then_inc(eps_done, 1)
                pool.wait_ge(eps_done, c)
                nc.gpsimd.tensor_tensor(r, r, half[:, :], ALU.pow).then_inc(rstd_done, 1)

            def add(dst, p, q, b, done):
                t = slice(b * QT, (b + 1) * QT)
                nc.gpsimd.tensor_tensor(dst[:, t, :], p[:, t, :], q, ALU.add).then_inc(done, 1)

            def vector(k):
                return spread[:, k:k + 1, :].to_broadcast([P, QT, D])

            for k in range(2):
                for b in range(B):
                    power(k, b)
            nc.gpsimd.memset(bdK[:, :, :, :, :], 0.0).then_inc(zero_set, 1)
            nc.gpsimd.memset(bdV[:, :, :, :, :], 0.0).then_inc(zero_set, 1)
            pool.wait_ge(spread_in, 16 * 5)
            for b in range(B):
                power(2, b)
            for b in range(B):
                pool.wait_ge(r1_done, b + 1)
                add(r1b, r1, vector(V_BO2), b, r1b_done)
            for b in range(B):
                add(r2b, x, vector(V_FB2), b, xr_done)
            for b in range(B):
                power(3, b)
                pool.wait_ge(xr_done, b + 1)
                pool.wait_ge(r2_done, QT * (b + 1))
                add(r2b, r2b, r2[:, b * QT:(b + 1) * QT, :], b, r2b_done)
            for b in range(B):
                power(4, b)
                pool.wait_ge(normed, QT * (2 * 4 + b + 1))
                add(tgtb, tgt, vector(V_EB2), b, tgtb_done)
            for b in range(B):
                power(5, b)
                t = slice(b * QT, (b + 1) * QT)
                pool.wait_ge(normed, QT * (2 * 5 + b + 1))
                nc.gpsimd.tensor_tensor(zn[:, t, :], zn[:, t, :], vector(V_GAMMA), ALU.mult).then_inc(zg_done, 1)
                pool.wait_ge(zg_done, b + 1)
                add(zn, zn, vector(V_BETA), b, zb_done)

        @block.scalar
        def _(act):
            act.dma_start(rows[R_COND:R_COND + 2, :], a["cond_1024"]).then_inc(rows_in, 16)
            for r, name, k in ((R_N1, "norm1_b", 2), (R_N2, "norm2_b", 2), (R_N3, "norm3_b", 2), (R_FB1, "ff_b1", 8)):
                act.dma_start(rows[r:r + k, :], a[pre + name].rearrange("(c p) -> c p", p=P)).then_inc(rows_in, 16)
            act.dma_start(rows[R_EB1:R_EB1 + FFC, :], a["L0_ffn_b1"][0].rearrange("(c p) -> c p", p=P)).then_inc(rows_in, 16)
            for k in range(3):
                act.dma_start(nw[:, k, :], a[pre + f"norm{k + 1}_w"]).then_inc(nw_in, 16)
            act.dma_start(bo1row[:, :, :], a[pre + "attn1_bo"].rearrange("(a c d) -> a c d", a=1, c=1).to_broadcast([1, QT, D])).then_inc(rows_in, 16)
            for k, v in ((V_FB2, a[pre + "ff_b2"]), (V_BO2, a[pre + "attn2_bo"]), (V_EB2, a["L0_ffn_b2"][0]),
                         (V_GAMMA, a["L0_ffn_gamma"]), (V_BETA, a["L0_ffn_beta"])):
                act.dma_start(spread[:, k, :], v.rearrange("(a d) -> a d", a=1).to_broadcast([P, D])).then_inc(spread_in, 16)

            def modulate(dst, k, b, count, src):
                act.wait_ge(mod_set, 6)
                act.wait_ge(turned, count)
                nc.scalar.activation(dst[:, b, :], src, ACT.Identity, bias=mod[:, k, 1, b:b + 1],
                                     scale=mod[:, k, 0, b:b + 1]).then_inc(hT_done, 1)

            for b in range(B):
                modulate(h1T, 0, b, b + 1, t_ps[b][:, :])

            def exp(i, first, s):
                g = i * STEPS + s
                for h in range(2):
                    act.wait_ge(maxed, 2 * g + h + 1)
                    if not (first and s < 2):
                        act.wait_ge(p_turned, 2 * (g - 2) + h + 1)
                    nc.scalar.activation(prob[:, s % 2, h, :], s_ps[h][:, :], ACT.Exp, bias=negmax[:, s % 2, h:h + 1],
                                         accum_out=psumr[:, s % 2, h:h + 1]).then_inc(exped, 1)

            def read_turned(i, first, s):
                g, b, q = i * STEPS + s, s // QT, s % QT
                if q == 0 and not first:
                    act.wait_ge(pv_done, 2 * i + b - 1)
                for h in range(2):
                    act.wait_ge(p_turned, 2 * g + h + 1)
                    nc.scalar.copy(PT[:, b, h, :, q * P:(q + 1) * P],
                                   t_ps[h][:, :].rearrange("p (c q) -> p c q", c=QT)).then_inc(p_read, 1)

            exp(0, True, 0)

            def body(i, first, last):
                for s in range(STEPS):
                    if s < STEPS - 1:
                        exp(i, first, s + 1)
                    elif not last:
                        exp(i + 1, False, 0)
                    read_turned(i, first, s)

            rounds(act, body)

            act.wait_ge(c_ps, 4)
            nc.scalar.mul(A2[:, :, 0:4, :], bank[4][:, :].rearrange("p (c b k) -> p b c k", c=4, b=B), SCALE).then_inc(c_read, 1)
            nc.scalar.mul(A2[:, :, 4:8, :], bank[5][:, :].rearrange("p (c b k) -> p b c k", c=4, b=B), SCALE).then_inc(c_read, 1)

            for b in range(B):
                modulate(h2T, 1, b, 2 + b + 1, y_ps[b][:, :])
            for t in range(NT):
                act.wait_ge(sub2_done, t + 1)
                nc.scalar.activation(e2[:, t % 2, :, :], e2[:, t % 2, :, :], ACT.Exp).then_inc(exp2_done, 1)
                act.wait_ge(t2_done, t + 1)
                if t >= 2:
                    act.wait_ge(out2_done, t - 1)
                nc.scalar.copy(PT2[:, t % 2, :, :], t_ps[t % 2][:, :].rearrange("p (c q) -> p c q", c=4)).then_inc(t2_read, 1)

            for b in range(B):
                modulate(h3T, 2, b, 4 + b + 1, y_ps[b][:, :])
                for c in range(FFC):
                    k = b * FFC + c
                    act.wait_ge(gate_ps, k + 1)
                    if k >= 2:
                        act.wait_ge(hid_done, k - 1)
                    nc.scalar.activation(gate[:, k % 2, :], s_ps[k % 2][:, :], ACT.Gelu,
                                         bias=cols[:, R_FB1 + FFC + c:R_FB1 + FFC + c + 1]).then_inc(gate_read, 1)
            for b in range(B):
                act.wait_ge(turned, 6 + b + 1)
                nc.scalar.copy(tT[:, b, :], y_ps[b][:, :]).then_inc(hT_done, 1)
                for c in range(FFC):
                    k = b * FFC + c
                    act.wait_ge(eh_ps, k + 1)
                    nc.scalar.activation(ehid[:, b, c, :], s_ps[k % 2][:, :], ACT.Relu,
                                         bias=cols[:, R_EB1 + c:R_EB1 + c + 1]).then_inc(eh_done, 1)

        @block.vector
        def _(dve):
            def layer_norm(k, b, src, dst):
                c = 2 * k + b
                for q in range(QT):
                    nc.vector.bn_stats(stats[:, b * QT + q, :], src[:, b * QT + q, :]).then_inc(stat_done, 1)
                for q in range(QT):
                    dve.wait_ge(stat_done, QT * c + q + 1)
                    nc.vector.bn_aggr(meanvar[:, k, b * QT + q, :], stats[:, b * QT + q, :]).then_inc(aggr_done, 1)

            def apply_norm(k, b, src, dst):
                c = 2 * k + b
                dve.wait_ge(rstd_done, c + 1)
                for q in range(QT):
                    t = b * QT + q
                    nc.vector.tensor_scalar(dst[:, t, :], src[:, t, :], meanvar[:, k, t, 0:1], rstd[:, k, t:t + 1],
                                            ALU.subtract, ALU.mult).then_inc(normed, 1)

            for b in range(B):
                dve.wait_ge(x_in[b], 16)
                layer_norm(0, b, x, xn)
            dve.wait_ge(cols_ps, 1)
            nc.vector.tensor_copy(cols[:, :], bank[6][:, 0:ROWS]).then_inc(cols_set, 1)
            for b in range(B):
                apply_norm(0, b, x, xn)
                dve.wait_ge(normed, QT * (b + 1))
                layer_norm(1, b, xn, n)
            dve.wait_ge(cols_set, 1)
            dve.wait_ge(mod_ps, 1)
            for k in range(3):
                for j in range(2):
                    col = cols[:, 2 + 2 * k + j:3 + 2 * k + j]
                    nc.vector.tensor_scalar(mod[:, k, j, :], bank[3][:, 4 * k + 2 * j:4 * k + 2 * j + 2], col,
                                            1.0 - j, ALU.add, ALU.add).then_inc(mod_set, 1)
            for b in range(B):
                apply_norm(1, b, xn, n)

            def read_projection(kind, b, h, count, first=False):
                dve.wait_ge(proj_done, count + 1)
                if kind == "W":
                    nc.vector.tensor_scalar(wqT[:, :], p_ps[:, 0:P], SCALE, None, ALU.mult)
                    nc.vector.tensor_copy(wkT[0:DH, 0, :], p_ps[0:DH, P:2 * P])
                    nc.vector.tensor_copy(wkT[DH:P, 1, :], p_ps[DH:P, P:2 * P]).then_inc(proj_read, 1)
                elif kind == "M":
                    nc.vector.tensor_copy(M[:, :, :], p_ps[:, 0:2 * P].rearrange("p (h d) -> p h d", h=2)).then_inc(proj_read, 1)
                elif kind == "G":
                    nc.vector.tensor_copy(G[:, b, h, :], p_ps[:, :]).then_inc(proj_read, 1)
                else:
                    nc.vector.tensor_copy(V[:, b, :, :], p_ps[:, :].rearrange("p (c d) -> p c d", c=QT)).then_inc(proj_read, 1)

            def row_max(i, s):
                g = i * STEPS + s
                for h in range(2):
                    dve.wait_ge(scored, 2 * g + h + 1)
                    nc.vector.tensor_reduce(negmax[:, s % 2, h:h + 1], s_ps[h][:, :], AX_X, ALU.max, negate=True).then_inc(maxed, 1)

            def normalise(i, s):
                g = i * STEPS + s
                for h in range(2):
                    dve.wait_ge(exped, 2 * g + h + 1)
                    nc.vector.reciprocal(rsum[:, s % 2, h:h + 1], psumr[:, s % 2, h:h + 1]).then_inc(summed, 1)
                for h in range(2):
                    dve.wait_ge(summed, 2 * g + h + 1)
                    nc.vector.tensor_scalar(prob[:, s % 2, h, :], prob[:, s % 2, h, :], rsum[:, s % 2, h:h + 1], None,
                                            ALU.mult).then_inc(probs_ready, 1)

            def read_o(u):
                dve.wait_ge(pv_done, u)
                nc.vector.tensor_copy(OT[:, :], o_ps[:, :]).then_inc(o_read, 1)

            dve.wait_ge(zero_set, 1)
            read_projection("W", 0, 0, 0)
            read_projection("M", 0, 0, 1)
            read_projection("G", 0, 0, 2)
            read_projection("G", 0, 1, 3)
            row_max(0, 0)
            normalise(0, 0)

            def body(i, first, last):
                ahead, behind = projections(i, last)
                for s in range(STEPS):
                    if s < STEPS - 1:
                        row_max(i, s + 1)
                    elif not last:
                        row_max(i + 1, 0)
                    if s in ahead:
                        read_projection(*ahead[s])
                    if s < STEPS - 1:
                        normalise(i, s + 1)
                    elif not last:
                        normalise(i + 1, 0)
                    if s in behind:
                        read_projection(*behind[s])
                    if s % QT == QT - 1 and not (first and s < QT):
                        u = 2 * i + s // QT
                        if not (first and s // QT <= 1):
                            dve.wait_ge(y_added, u - 1)
                        read_o(u)

            rounds(dve, body)
            dve.wait_ge(y_added, 2 * PAIRS - 1)
            read_o(2 * PAIRS)

            dve.wait_ge(zero_set, 3)
            for m, (dst, ps) in enumerate(((bdK, s_ps[0]), (bdV, s_ps[1]))):
                if m == 0:
                    dve.wait_ge(c_ps, 1)
                    nc.vector.tensor_copy(ctxT[:, :], bank[4][:, 0:B * CTX]).then_inc(c_read, 1)
                    dve.wait_ge(c_ps, 2)
                    nc.vector.tensor_copy(wq2T[:, 0:4, :], o_ps[:, :].rearrange("p (c d) -> p c d", c=4))
                    nc.vector.tensor_copy(wq2T[:, 4:8, :], p_ps[:, :].rearrange("p (c d) -> p c d", c=4)).then_inc(c_read, 1)
                    dve.wait_ge(c_ps, 3)
                v = ps[:, :].rearrange("p (c b k) -> p c b k", c=PAIRS, b=B)
                nc.vector.tensor_copy(dst[0:DH, :, :, 0, :], v[0:DH])
                nc.vector.tensor_copy(dst[DH:P, :, :, 1, :], v[DH:P]).then_inc(c_read, 1)
            for b in range(B):
                dve.wait_ge(y_added, 2 * PAIRS - 1 + b)
                t = slice(b * QT, (b + 1) * QT)
                nc.vector.tensor_tensor(r1[:, t, :], y_ps[b][:, :].rearrange("p (q d) -> p q d", q=QT), xn[:, t, :],
                                        ALU.add).then_inc(r1_done, 1)
                dve.wait_ge(r1_done, b + 1)
                layer_norm(2, b, r1, n)
            dve.wait_ge(c_ps, 5)
            for b in range(B):
                nc.vector.tensor_copy(B2[:, b, :, :], (o_ps, p_ps)[b][:, :].rearrange("p (c d) -> p c d", c=4)).then_inc(c_read, 1)
            for b in range(B):
                apply_norm(2, b, r1, n)

            def scores2(t):
                dve.wait_ge(sc2_done, t + 1)
                sc = s_ps[t % 2][:, :].rearrange("p (h k) -> p h k", h=H)
                nc.vector.tensor_reduce(m2[:, t % 2, :], sc, AX_X, ALU.max).then_inc(max2_done, 1)
                dve.wait_ge(max2_done, t + 1)
                if t >= 2:
                    dve.wait_ge(t2_done, t - 1)
                nc.vector.tensor_tensor(e2[:, t % 2, :, :], sc, m2[:, t % 2, :].to_broadcast([P, H, CTX]),
                                        ALU.subtract).then_inc(sub2_done, 1)

            def probs2(t):
                dve.wait_ge(exp2_done, t + 1)
                nc.vector.tensor_reduce(s2[:, t % 2, :], e2[:, t % 2, :, :], AX_X, ALU.add).then_inc(sum2_done, 1)
                dve.wait_ge(sum2_done, t + 1)
                nc.vector.reciprocal(i2[:, t % 2, :], s2[:, t % 2, :]).then_inc(inv2_done, 1)
                dve.wait_ge(inv2_done, t + 1)
                nc.vector.tensor_tensor(e2[:, t % 2, :, :], e2[:, t % 2, :, :],
                                        i2[:, t % 2, :].to_broadcast([P, H, CTX]), ALU.mult).then_inc(nrm2_done, 1)

            def join2(t):
                dve.wait_ge(out2_done, t + 1)
                dve.wait_ge(r1b_done, t // QT + 1)
                nc.vector.tensor_tensor(r2[:, t, :], bank[6 + t % 2][:, 0:D], r1b[:, t, :], ALU.add).then_inc(r2_done, 1)

            scores2(0)
            for t in range(NT):
                if t + 1 < NT:
                    scores2(t + 1)
                probs2(t)
                if t >= 1:
                    join2(t - 1)
                if t - 1 == QT - 1:
                    dve.wait_ge(r2_done, QT)
                    layer_norm(3, 0, r2, n)
                    apply_norm(3, 0, r2, n)
            join2(NT - 1)
            dve.wait_ge(r2_done, NT)
            layer_norm(3, 1, r2, n)
            apply_norm(3, 1, r2, n)

            def join(b, ps, count, sem_ps, other, other_done, dst, done):
                t = slice(b * QT, (b + 1) * QT)
                dve.wait_ge(sem_ps, count)
                dve.wait_ge(other_done, b + 1)
                nc.vector.tensor_tensor(dst[:, t, :], ps[:, :].rearrange("p (q d) -> p q d", q=QT), other[:, t, :],
                                        ALU.add).then_inc(done, 1)

            for b in range(B):
                for c in range(FFC):
                    k = b * FFC + c
                    dve.wait_ge(lin_ps, k + 1)
                    dve.wait_ge(gate_read, k + 1)
                    nc.vector.scalar_tensor_tensor(out=hid[:, b, c, :], in0=t_ps[k % 2][:, :],
                                                   scalar=cols[:, R_FB1 + c:R_FB1 + c + 1], in1=gate[:, k % 2, :],
                                                   op0=ALU.add, op1=ALU.mult).then_inc(hid_done, 1)
            for b in range(B):
                join(b, bank[6 + b], b + 1, ff_ps, r2b, r2b_done, r3, r3_done)
                dve.wait_ge(r3_done, b + 1)
                layer_norm(4, b, r3, tgt)
                apply_norm(4, b, r3, tgt)
            for b in range(B):
                join(b, bank[6 + b], b + 1, e_ps, tgtb, tgtb_done, z, z_done)
                dve.wait_ge(z_done, b + 1)
                layer_norm(5, b, z, zn)
                apply_norm(5, b, z, zn)
            for b in range(B):
                t = slice(b * QT, (b + 1) * QT)
                dve.wait_ge(zb_done, b + 1)
                nc.vector.tensor_tensor(res[:, t, :], r3[:, t, :], zn[:, t, :], ALU.add).then_inc(res_done, 1)

        @block.tensor
        def _(pe):
            mm = nc.tensor.matmul

            def turn(src, b, dst):
                for q in range(QT):
                    last = nc.tensor.transpose(dst[:, q * P:(q + 1) * P], src[:, b * QT + q, :], ident[:, :])
                last.then_inc(turned, 1)

            pe.wait_ge(ident_done, 1)
            pe.wait_ge(rows_in, 16 * 7)
            nc.tensor.transpose(bank[6][:, 0:ROWS], rows[:, :], ident[0:ROWS, 0:ROWS]).then_inc(cols_ps, 1)
            pe.wait_ge(stage_in, 32)
            for m in range(2):
                last = nc.tensor.transpose(p_ps[:, m * P:(m + 1) * P], stage[:, m, :], ident[:, :])
            last.then_inc(proj_done, 1)
            pe.wait_ge(cols_set, 1)
            pe.wait_ge(nw_in, 48)
            for k in range(3):
                for j in range(2):
                    last = mm(bank[3][:, 4 * k + 2 * j:4 * k + 2 * j + 2], nw[:, k, j * D:(j + 1) * D],
                              cols[:, R_COND:R_COND + 2], start=True, stop=True)
            last.then_inc(mod_ps, 1)
            for b in range(B):
                mm(y_ps[b][:, :], ones[:, :], bo1row[:, :, :], start=True, stop=False, skip_group_check=True)
            for b in range(B):
                pe.wait_ge(normed, QT * (2 + b + 1))
                turn(n, b, t_ps[b])

            def project(kind, b, h, count, i, first=False):
                pe.wait_ge(proj_read, count)
                if kind == "W":
                    pe.wait_ge(stage_in, 32 * (i + 2))
                    for m in range(2):
                        last = nc.tensor.transpose(p_ps[:, m * P:(m + 1) * P], stage[:, m, :], ident[:, :])
                elif kind == "M":
                    last = mm(p_ps[:, 0:2 * P], wqT[:, :], wkT[:, :, :], start=True, stop=True)
                elif kind == "G":
                    last = mm(p_ps[:, :], M[:, h, :], h1T[:, b, :], start=True, stop=True)
                else:
                    for c in range(QT):
                        last = mm(p_ps[:, c * P:(c + 1) * P], h1T[:, b, c * P:(c + 1) * P], wv[:, ds(i * P, P)],
                                  start=True, stop=True)
                last.then_inc(proj_done, 1)

            def scores(i, first, s):
                g, b, q = i * STEPS + s, s // QT, s % QT
                for h in range(2):
                    if not (first and s == 0):
                        pe.wait_ge(exped, 2 * (g - 1) + h + 1)
                    mm(s_ps[h][:, :], G[:, b, h, q * P:(q + 1) * P], h1T[:, b, :], start=True, stop=True).then_inc(scored, 1)

            def turn_probs(i, first, s):
                g = i * STEPS + s
                for h in range(2):
                    pe.wait_ge(probs_ready, 2 * g + h + 1)
                    if not (first and s == 0):
                        pe.wait_ge(p_read, 2 * (g - 1) + h + 1)
                    for c in range(QT):
                        last = nc.tensor.transpose(t_ps[h][:, c * P:(c + 1) * P], prob[:, s % 2, h, c * P:(c + 1) * P], ident[:, :])
                    last.then_inc(p_turned, 1)

            def times_v(b, c):
                for h in range(2):
                    last = mm(o_ps[h * DH:(h + 1) * DH, :], V[:, b, c, h * DH:(h + 1) * DH], PT[:, b, h, c, :],
                              start=(c == 0), stop=(c == QT - 1), skip_group_check=True)
                if c == QT - 1:
                    last.then_inc(pv_done, 1)

            def add_y(b, pair, u):
                pe.wait_ge(o_read, u + 1)
                for q in range(QT):
                    last = mm(y_ps[b][:, q * P:(q + 1) * P], OT[:, q * P:(q + 1) * P],
                              wo[:, pair, :] if isinstance(pair, int) else wo[:, ds(pair, 1), :],
                              start=False, stop=False, skip_group_check=True)
                last.then_inc(y_added, 1)

            pe.wait_ge(proj_read, 1)
            mm(p_ps[:, 0:2 * P], wqT[:, :], wkT[:, :, :], start=True, stop=True).then_inc(proj_done, 1)
            pe.wait_ge(hT_done, 2)
            for h in range(2):
                pe.wait_ge(proj_read, 2 + h)
                mm(p_ps[:, :], M[:, h, :], h1T[:, 0, :], start=True, stop=True).then_inc(proj_done, 1)
            pe.wait_ge(proj_read, 4)
            scores(0, True, 0)
            pe.wait_ge(wv_in, 16)
            pe.wait_ge(wo_in, 16)

            def body(i, first, last):
                ahead, behind = projections(i, last)
                for s in range(STEPS):
                    b, q = s // QT, s % QT
                    if s == QT - 1:
                        pe.wait_ge(proj_read, ahead[1][3] + 1)
                    if s < STEPS - 1:
                        scores(i, first, s + 1)
                    elif not last:
                        pe.wait_ge(proj_read, ahead[5][3] + 1)
                        scores(i + 1, False, 0)
                    if s in ahead:
                        project(*ahead[s], i)
                    turn_probs(i, first, s)
                    if s in behind:
                        project(*behind[s], i)
                    u = 2 * i + b
                    if q == 0 and not (first and b == 0):
                        if not (first and b == 1):
                            add_y(b, i - 1, u - 2)
                            pe.wait_ge(o_read, u - 1)
                        pe.wait_ge(p_read, 2 * QT * u)
                        if b == 0:
                            pe.wait_ge(proj_read, ahead[0][3])
                        else:
                            pe.wait_ge(proj_read, ahead[3][3] + 1)
                    if not (first and b == 0):
                        times_v(1 - b, q)

            rounds(pe, body)
            add_y(0, PAIRS - 1, 2 * PAIRS - 2)
            pe.wait_ge(p_read, 2 * QT * 2 * PAIRS)
            pe.wait_ge(proj_read, (PAIRS - 1) * PROJ_ROUND + PROJ_BEFORE + 4)
            for c in range(QT):
                times_v(1, c)

            pe.wait_ge(w2_in, 16 * 5)
            nc.tensor.transpose(bank[4][:, 0:B * CTX], ctxt[:, :], ident[0:B * CTX, 0:B * CTX]).then_inc(c_ps, 1)
            add_y(1, PAIRS - 1, 2 * PAIRS - 1)
            for c in range(PAIRS):
                last = nc.tensor.transpose((o_ps, p_ps)[c // 4][:, (c % 4) * P:(c % 4 + 1) * P],
                                           wq2[:, c * P:(c + 1) * P], ident[:, :])
            last.then_inc(c_ps, 1)
            pe.wait_ge(c_read, 1)
            for w, ps in ((wk2, s_ps[0]), (wv2, s_ps[1])):
                for c in range(PAIRS):
                    last = mm(ps[:, c * 64:(c + 1) * 64], w[:, c * P:(c + 1) * P], ctxT[:, :], start=True, stop=True)
            last.then_inc(c_ps, 1)
            pe.wait_ge(c_read, 4)
            for c in range(PAIRS):
                last = mm(bank[4 + c // 4][:, (c % 4) * P:(c % 4 + 1) * P], wq2T[:, c, :], bdK[:, c, :, :, :],
                          start=True, stop=True)
            last.then_inc(c_ps, 1)
            for b in range(B):
                for c in range(PAIRS):
                    last = mm((o_ps, p_ps)[b][(c % 2) * DH:(c % 2 + 1) * DH, (c // 2) * D:(c // 2 + 1) * D],
                              bdV[:, c, b, :, :], wo2[:, c, :], start=True, stop=True)
            last.then_inc(c_ps, 1)

            for b in range(B):
                pe.wait_ge(normed, QT * (2 * 2 + b + 1))
                turn(n, b, y_ps[b])
            pe.wait_ge(c_read, 8)

            def scores_2(t):
                if t >= 2:
                    pe.wait_ge(sub2_done, t - 1)
                pe.wait_ge(hT_done, 2 + t // QT + 1)
                mm(s_ps[t % 2][:, :], h2T[:, t // QT, (t % QT) * P:(t % QT + 1) * P], A2[:, t // QT, :, :],
                   start=True, stop=True).then_inc(sc2_done, 1)

            scores_2(0)
            scores_2(1)
            for t in range(NT):
                pe.wait_ge(nrm2_done, t + 1)
                if t >= 2:
                    pe.wait_ge(t2_read, t - 1)
                for c in range(4):
                    last = nc.tensor.transpose(t_ps[t % 2][:, c * P:(c + 1) * P], e2[:, t % 2, 4 * c:4 * c + 4, :], ident[:, :])
                last.then_inc(t2_done, 1)
                if t + 2 < NT:
                    scores_2(t + 2)
                pe.wait_ge(t2_read, t + 1)
                if t >= 2:
                    pe.wait_ge(r2_done, t - 1)
                for c in range(4):
                    last = mm(bank[6 + t % 2][:, 0:D], PT2[:, t % 2, c, :], B2[:, t // QT, c, :],
                              start=(c == 0), stop=(c == 3))
                last.then_inc(out2_done, 1)

            def down(b, w, hidden, done):
                for q in range(QT):
                    for c in range(FFC):
                        last = mm(bank[6 + b][:, q * P:(q + 1) * P], hidden[:, b, c, q * P:(q + 1) * P], w[:, c, :],
                                  start=(c == 0), stop=(c == FFC - 1))
                last.then_inc(done, 1)

            pe.wait_ge(ff_in, 32)
            for b in range(B):
                pe.wait_ge(normed, QT * (2 * 3 + b + 1))
                turn(n, b, y_ps[b])
                pe.wait_ge(hT_done, 4 + b + 1)
                for c in range(FFC):
                    k = b * FFC + c
                    if k >= 2:
                        pe.wait_ge(gate_read, k - 1)
                    mm(s_ps[k % 2][:, :], fw1[:, DFF + c * P:DFF + (c + 1) * P], h3T[:, b, :], start=True, stop=True).then_inc(gate_ps, 1)
                    if k >= 2:
                        pe.wait_ge(hid_done, k - 1)
                    mm(t_ps[k % 2][:, :], fw1[:, c * P:(c + 1) * P], h3T[:, b, :], start=True, stop=True).then_inc(lin_ps, 1)
            pe.wait_ge(r2_done, NT)
            for b in range(B):
                pe.wait_ge(hid_done, FFC * (b + 1))
                down(b, fw2, hid, ff_ps)
            pe.wait_ge(ew_in, 32)
            for b in range(B):
                pe.wait_ge(normed, QT * (2 * 4 + b + 1))
                turn(tgt, b, y_ps[b])
                pe.wait_ge(hT_done, 6 + b + 1)
                for c in range(FFC):
                    k = b * FFC + c
                    if k >= 2:
                        pe.wait_ge(eh_done, k - 1)
                    mm(s_ps[k % 2][:, :], ew1[:, c * P:(c + 1) * P], tT[:, b, :], start=True, stop=True).then_inc(eh_ps, 1)
            for b in range(B):
                pe.wait_ge(eh_done, FFC * (b + 1))
                pe.wait_ge(r3_done, b + 1)
                down(b, ew2, ehid, e_ps)


_X = "L0_xcond_"
_INS = (["x", "cond_1024", "ctx_1024"] + [_X + f"attn{k}_{w}" for k in (1, 2) for w in ("wq", "wk", "wv", "wo", "bo")]
        + [_X + w for w in ("ff_w1", "ff_b1", "ff_w2", "ff_b2")] + [_X + f"norm{k}_{w}" for k in (1, 2, 3) for w in "wb"]
        + ["L0_ffn_" + w for w in ("w1", "b1", "w2", "b2", "gamma", "beta")])


def kernel(**inputs):
    import numpy as _np
    import concourse.bacc as _bacc
    from concourse import mybir as _mybir
    from concourse.bass_utils import run_bass_kernel_spmd as _run

    nc = _bacc.Bacc("TRN2", target_bir_lowering=False, num_devices=1)
    arrays, args = {}, {}
    for name in _INS:
        v = _np.ascontiguousarray(inputs[name])
        arrays[f"in_{name}"] = v
        args[name] = nc.dram_tensor(f"in_{name}", v.shape, _mybir.dt.from_np(v.dtype), kind="ExternalInput").ap()
    out = nc.dram_tensor("out_0", (B, S, D), F32, kind="ExternalOutput").ap()
    residual_block(nc, args, out)
    r = _run(nc, [arrays], core_ids=[0])
    return r.results[0]["out_0"]
```

```python
from contextlib import ExitStack

import concourse.bass as bass
from concourse import mybir

F32 = mybir.dt.float32
F32R = mybir.dt.float32r
ALU = mybir.AluOpType
ACT = mybir.ActivationFunctionType
AX_X = mybir.AxisListType.X
ds = bass.ds

P = 128
B, S, D, H, DH, CTX = 2, 512, 128, 16, 64, 32
QT = S // P
NT = B * QT
PAIRS = H // 2
STEPS = B * QT
DFF = 4 * D
FFC = DFF // P
SCALE = 1.0 / 8.0
EPS = 1e-5
NLN = 6
NE = 3

R_COND, R_N1, R_N2, R_N3, R_FB1, R_EB1 = 0, 2, 4, 6, 8, 16
ROWS = 20
V_FB2, V_BO2, V_EB2, V_GAMMA, V_BETA = range(5)


def residual_block(nc, a, out):
    x_d = a["x"].rearrange("b (t p) d -> p (b t) d", p=P)
    out_d = out.rearrange("b (t p) d -> p (b t) d", p=P)
    pre = "L0_xcond_"
    wq_d, wk_d, wv_d = (a[pre + f"attn1_w{c}"] for c in "qkv")
    wo_d = a[pre + "attn1_wo"].rearrange("(c p) d -> p c d", p=P)
    wo2_d = a[pre + "attn2_wo"].rearrange("(c p) d -> p c d", p=P)
    fw2_d = a[pre + "ff_w2"].rearrange("(c p) d -> p c d", p=P)
    ew1_d = a["L0_ffn_w1"][0]
    ew2_d = a["L0_ffn_w2"][0].rearrange("(c p) d -> p c d", p=P)

    with ExitStack() as ctx:
        def sb(name, *shape, dt=F32):
            return ctx.enter_context(nc.sbuf_tensor(name, list(shape), dt))

        def sem(name):
            return ctx.enter_context(nc.semaphore(name))

        x = sb("x", P, NT, D)
        xn = sb("xn", P, NT, D)
        n = sb("n", P, NT, D)
        r2b = sb("r2b", P, NT, D)
        stats = sb("stats", P, NT, 6)
        meanvar = sb("meanvar", P, NLN, NT, 2)
        rstd = sb("rstd", P, NLN, NT)
        half = sb("half", P, QT)
        warm = sb("warm", P, 2)
        ident = sb("ident", P, P)
        ones = sb("ones", 1, P)
        rows = sb("rows", ROWS, P)
        cols = sb("cols", P, ROWS)
        spread = sb("spread", P, 5, D)
        bo1row = sb("bo1row", 1, QT, D)
        nw = sb("nw", P, 3, 2 * D)
        mod = sb("mod", P, 3, 2, B)
        h1T = sb("h1T", P, B, S)
        h1hi = sb("h1hi", P, B, S, dt=F32R)
        h1lo = sb("h1lo", P, B, S, dt=F32R)
        stage = sb("stage", P, 2, P)
        wv = sb("wv", P, H * DH)
        wo = sb("wo", P, PAIRS, D)
        wqT = sb("wqT", P, P)
        wkT = sb("wkT", P, 2, P)
        Mhi = sb("Mhi", P, 2, P, dt=F32R)
        Mlo = sb("Mlo", P, 2, P, dt=F32R)
        Ghi = sb("Ghi", P, B, 2, S, dt=F32R)
        Glo = sb("Glo", P, B, 2, S, dt=F32R)
        V = sb("V", P, B, QT, 2 * DH)
        prob = sb("prob", P, 2, 2, S)
        negmax = sb("negmax", P, 2, 2)
        psumr = sb("psumr", P, 2, 2)
        rsum = sb("rsum", P, 2, 2)
        PT = sb("PT", P, B, 2, QT, S)
        OT = sb("OT", P, S)
        ctxt = sb("ctxt", B * CTX, D)
        ctxT = sb("ctxT", P, B * CTX)
        wq2 = sb("wq2", P, H * DH)
        wk2 = sb("wk2", P, H * DH)
        wv2 = sb("wv2", P, H * DH)
        wo2 = sb("wo2", P, PAIRS, D)
        wq2T = sb("wq2T", P, PAIRS, P)
        bdK = sb("bdK", P, PAIRS, B, 2, CTX)
        bdV = sb("bdV", P, PAIRS, B, 2, CTX)
        A2 = sb("A2", P, B, PAIRS, 2 * CTX)
        B2 = sb("B2", P, B, 4, D)
        e2 = sb("e2", P, NE, H, CTX)
        m2 = sb("m2", P, NE, H)
        s2 = sb("s2", P, NE, H)
        i2 = sb("i2", P, NE, H)
        PT2 = sb("PT2", P, 2, 4, P)
        fw1 = sb("fw1", P, 2 * DFF)
        fw2 = sb("fw2", P, FFC, D)
        ew1 = sb("ew1", P, DFF)
        ew2 = sb("ew2", P, FFC, D)

        r1 = wq2[:, :].rearrange("p (t d) -> p t d", d=D)
        r1b = wk2[:, :].rearrange("p (t d) -> p t d", d=D)
        r2 = wv2[:, :].rearrange("p (t d) -> p t d", d=D)
        r3 = wo2[:, :, :]
        tgt = wq2T[:, :, :]
        tgtb = bdK[:, :, :, :, :].rearrange("p t b h k -> p t (b h k)")
        z = bdV[:, :, :, :, :].rearrange("p t b h k -> p t (b h k)")
        h2T, h3T = prob[:, 0, :, :], prob[:, 1, :, :]
        tT, gate = h1T, V[:, :, :, :].rearrange("p b c d -> p b (c d)")
        zn = wv[:, :].rearrange("p (t d) -> p t d", d=D)
        hid = PT[:, :, 0, :, :]
        ehid = PT[:, :, 1, :, :]

        bank = [ctx.enter_context(nc.psum_tensor(f"bank{k}", [P, 512], F32)) for k in range(8)]
        y_ps = bank[0:2]
        s_ps = bank[2:4]
        t_ps = bank[4:6]
        o_ps = bank[6]
        p_ps = bank[7]

        x_in = [sem("x_in0"), sem("x_in1")]
        rows_in, nw_in, spread_in = sem("rows_in"), sem("nw_in"), sem("spread_in")
        stage_in, wv_in, wo_in = sem("stage_in"), sem("wv_in"), sem("wo_in")
        ctx_in, wq2_in, wk2_in, wv2_in, wo2_in = (sem(v) for v in ("ctx_in", "wq2_in", "wk2_in", "wv2_in", "wo2_in"))
        bo1_in, ff_in, ew_in = sem("bo1_in"), sem("ff_in"), sem("ew_in")
        stored = sem("stored")
        const_set, ident_done, zero_set = sem("const_set"), sem("ident_done"), sem("zero_set")
        cols_ps, cols_set, mod_ps, mod_set = sem("cols_ps"), sem("cols_set"), sem("mod_ps"), sem("mod_set")
        stat_done, aggr_done, eps_done = sem("stat_done"), sem("aggr_done"), sem("eps_done")
        rstd_done, normed = sem("rstd_done"), sem("normed")
        turned, hT_done, h1_split = sem("turned"), sem("hT_done"), sem("h1_split")
        proj_done, hi_done, proj_read = sem("proj_done"), sem("hi_done"), sem("proj_read")
        scored, maxed, exped = sem("scored"), sem("maxed"), sem("exped")
        summed, probs_ready = sem("summed"), sem("probs_ready")
        p_turned, p_read = sem("p_turned"), sem("p_read")
        pv_done, o_read, y_added = sem("pv_done"), sem("o_read"), sem("y_added")
        c_ps, c_read = sem("c_ps"), sem("c_read")
        sc2_done, max2_done, sub2_done = sem("sc2_done"), sem("max2_done"), sem("sub2_done")
        exp2_done, sum2_done, inv2_done, nrm2_done = sem("exp2_done"), sem("sum2_done"), sem("inv2_done"), sem("nrm2_done")
        t2_done, t2_read, out2_done = sem("t2_done"), sem("t2_read"), sem("out2_done")
        r1_done, r1b_done, r2_done, r2b_done = sem("r1_done"), sem("r1b_done"), sem("r2_done"), sem("r2b_done")
        r3_done, r3b_done, tgtb_done, z_done, zg_done = sem("r3_done"), sem("r3b_done"), sem("tgtb_done"), sem("z_done"), sem("zg_done")
        xr_done = sem("xr_done")
        res_done = sem("res_done")
        gate_ps, gate_read, lin_ps, hid_done = sem("gate_ps"), sem("gate_read"), sem("lin_ps"), sem("hid_done")
        ff_ps, eh_ps, eh_done, e_ps = sem("ff_ps"), sem("eh_ps"), sem("eh_done"), sem("e_ps")

        PROJ_BEFORE = 4
        PROJ_ROUND = 8
        HI_BEFORE, HI_ROUND = 3, 5
        PREP = {0: ("ctx", "wq0", "wq1"), 1: ("K", "V"), 2: ("A0", "A1"), 3: ("B0", "B1")}
        PREP_ORDER = [e for s in range(QT) for e in PREP[s]]

        def projections(i, last):
            c = i * PROJ_ROUND + PROJ_BEFORE
            v = i * HI_ROUND + HI_BEFORE
            ahead = {0: ("G", 1, 0, c, v), 1: ("G", 1, 1, c + 1, v + 1), 2: ("W", 0, 0, c + 2, 0), 3: ("V", 0, 0, c + 4, 0),
                     4: ("G", 0, 0, c + 5, v + 3), 5: ("G", 0, 1, c + 6, v + 4), 6: ("V", 1, 0, c + 7, 0)}
            behind = {2: ("M", 0, 0, c + 3, v + 2)}
            if last:
                ahead = {0: ahead[0], 1: ahead[1], 3: ("V", 0, 0, c + 2, 0), 6: ("V", 1, 0, c + 3, 0)}
                behind = {}
            return ahead, behind

        def prep_of(first, s, slot):
            return PREP[s][slot:slot + 1] if first and s in PREP else ()

        def e_bank(m):
            return bank[6 + m // 2 - 2 * (m % 2)]

        def rounds(eng, body):
            body(0, True, False)
            with eng.Fori(1, PAIRS - 1) as i:
                body(i, False, False)
            body(PAIRS - 1, False, True)

        block = ctx.enter_context(nc.Block())

        @block.sync
        def _(sp):
            sp.dma_start(x[:, 0:QT, :], x_d[:, 0:QT, :]).then_inc(x_in[0], 16)
            sp.dma_start(stage[:, 0, :], wq_d[:, 0:P]).then_inc(stage_in, 16)
            sp.dma_start(stage[:, 1, :], wk_d[:, 0:P]).then_inc(stage_in, 16)
            sp.dma_start(x[:, QT:NT, :], x_d[:, QT:NT, :]).then_inc(x_in[1], 16)
            sp.dma_start(wv[:, :], wv_d).then_inc(wv_in, 16)
            sp.dma_start(ctxt[:, :], a["ctx_1024"].rearrange("b c d -> (b c) d")).then_inc(ctx_in, 16)
            sp.dma_start(wq2[:, :], a[pre + "attn2_wq"]).then_inc(wq2_in, 16)
            sp.dma_start(wk2[:, :], a[pre + "attn2_wk"]).then_inc(wk2_in, 16)
            sp.dma_start(wv2[:, :], a[pre + "attn2_wv"]).then_inc(wv2_in, 16)
            sp.wait_ge(proj_done, 1)
            sp.dma_start(stage[:, 0, :], wq_d[:, P:2 * P]).then_inc(stage_in, 16)
            sp.dma_start(stage[:, 1, :], wk_d[:, P:2 * P]).then_inc(stage_in, 16)
            sp.dma_start(wo2[:, :, :], wo2_d).then_inc(wo2_in, 16)
            sp.dma_start(wo[:, :, :], wo_d).then_inc(wo_in, 16)
            sp.dma_start(fw1[:, :], a[pre + "ff_w1"]).then_inc(ff_in, 16)
            sp.dma_start(fw2[:, :, :], fw2_d).then_inc(ff_in, 16)
            sp.dma_start(ew1[:, :], ew1_d).then_inc(ew_in, 16)
            sp.dma_start(ew2[:, :, :], ew2_d).then_inc(ew_in, 16)
            with sp.Fori(1, PAIRS - 1) as i:
                sp.wait_ge(proj_done, i * PROJ_ROUND + PROJ_BEFORE + 3 - PROJ_ROUND)
                sp.dma_start(stage[:, 0, :], wq_d[:, ds((i + 1) * P, P)]).then_inc(stage_in, 16)
                sp.dma_start(stage[:, 1, :], wk_d[:, ds((i + 1) * P, P)]).then_inc(stage_in, 16)
            for m in range(2 * B):
                sp.wait_ge(res_done, m + 1)
                sp.dma_start(out_d[:, 2 * m:2 * m + 2, :], zn[:, 2 * m:2 * m + 2, :]).then_inc(stored, 16)
            sp.wait_ge(stored, 16 * 2 * B)

        @block.gpsimd
        def _(pool):
            nc.gpsimd.memset(ident[:, :], 0.0).then_inc(const_set, 1)
            nc.gpsimd.memset(half[:, :], -0.5).then_inc(const_set, 1)
            nc.gpsimd.memset(ones[:, :], 1.0).then_inc(const_set, 1)
            pool.wait_ge(const_set, 3)
            nc.gpsimd.affine_select(out=ident[:, :], in_=ident[:, :], compare_op=ALU.not_equal, fill=1.0,
                                    base=0, pattern=[[-1, P]], channel_multiplier=1).then_inc(ident_done, 1)
            nc.gpsimd.memset(wkT[:, :, :], 0.0).then_inc(zero_set, 1)

            def power(k, t0, nt, aggr, c):
                r = rstd[:, k, t0:t0 + nt]
                pool.wait_ge(aggr_done, aggr)
                nc.gpsimd.tensor_scalar(r, meanvar[:, k, t0:t0 + nt, 1], EPS, None, ALU.add).then_inc(eps_done, 1)
                pool.wait_ge(eps_done, c)
                nc.gpsimd.tensor_tensor(r, r, half[:, 0:nt], ALU.pow).then_inc(rstd_done, 1)

            def batch_power(k, b):
                power(k, b * QT, QT, QT * (2 * k + b + 1), 2 * k + b + 1)

            def batch(t, b):
                return t[:, b * QT:(b + 1) * QT, :]

            def vector(k):
                return spread[:, k:k + 1, :].to_broadcast([P, QT, D])

            for k in range(2):
                for b in range(B):
                    batch_power(k, b)
            nc.gpsimd.memset(bdK[:, :, :, :, :], 0.0).then_inc(zero_set, 1)
            nc.gpsimd.memset(bdV[:, :, :, :, :], 0.0).then_inc(zero_set, 1)
            pool.wait_ge(spread_in, 16 * 5)
            for b in range(B):
                nc.gpsimd.tensor_tensor(batch(r2b, b), batch(x, b), vector(V_FB2), ALU.add).then_inc(xr_done, 1)

            def add_bias2(b):
                pool.wait_ge(r1_done, b + 1)
                nc.gpsimd.tensor_tensor(batch(r1b, b), batch(r1, b), vector(V_BO2), ALU.add).then_inc(r1b_done, 1)

            def normalise2(t):
                pool.wait_ge(inv2_done, t + 1)
                nc.gpsimd.tensor_tensor(e2[:, t % NE, :, :], e2[:, t % NE, :, :],
                                        i2[:, t % NE, :].to_broadcast([P, H, CTX]), ALU.mult).then_inc(nrm2_done, 1)

            def add_r2(b):
                pool.wait_ge(xr_done, b + 1)
                pool.wait_ge(r2_done, QT * (b + 1))
                nc.gpsimd.tensor_tensor(batch(r2b, b), batch(r2b, b), batch(r2, b), ALU.add).then_inc(r2b_done, 1)

            batch_power(2, 0)
            batch_power(2, 1)
            add_bias2(0)
            for t in range(NT):
                normalise2(t)
                if t == 1:
                    add_bias2(1)
                if t == QT + 1:
                    batch_power(3, 0)
                    add_r2(0)
            batch_power(3, 1)
            add_r2(1)
            for b in range(B):
                batch_power(4, b)
                pool.wait_ge(normed, QT * (2 * 4 + b + 1))
                nc.gpsimd.tensor_tensor(batch(tgtb, b), batch(tgt, b), vector(V_EB2), ALU.add).then_inc(tgtb_done, 1)
                nc.gpsimd.tensor_tensor(batch(r1, b), batch(r3, b), vector(V_BETA), ALU.add).then_inc(r3b_done, 1)
            for m in range(2 * B):
                power(5, 2 * m, 2, QT * 2 * 5 + 2 * (m + 1), 2 * 5 + m + 1)

        @block.scalar
        def _(act):
            act.dma_start(rows[R_COND:R_COND + 2, :], a["cond_1024"]).then_inc(rows_in, 16)
            for r, name, k in ((R_N1, "norm1_b", 2), (R_N2, "norm2_b", 2), (R_N3, "norm3_b", 2), (R_FB1, "ff_b1", 8)):
                act.dma_start(rows[r:r + k, :], a[pre + name].rearrange("(c p) -> c p", p=P)).then_inc(rows_in, 16)
            act.dma_start(rows[R_EB1:R_EB1 + FFC, :], a["L0_ffn_b1"][0].rearrange("(c p) -> c p", p=P)).then_inc(rows_in, 16)
            for k in range(3):
                act.dma_start(nw[:, k, :], a[pre + f"norm{k + 1}_w"]).then_inc(nw_in, 16)
            act.dma_start(bo1row[:, :, :], a[pre + "attn1_bo"].rearrange("(a c d) -> a c d", a=1, c=1).to_broadcast([1, QT, D])).then_inc(bo1_in, 16)
            for k, v in ((V_FB2, a[pre + "ff_b2"]), (V_BO2, a[pre + "attn2_bo"]), (V_EB2, a["L0_ffn_b2"][0]),
                         (V_GAMMA, a["L0_ffn_gamma"]), (V_BETA, a["L0_ffn_beta"])):
                act.dma_start(spread[:, k, :], v.rearrange("(a d) -> a d", a=1).to_broadcast([P, D])).then_inc(spread_in, 16)
            act.wait_ge(const_set, 3)
            nc.scalar.activation(warm[:, 0:1], half[:, 0:1], ACT.Exp)

            def modulate(dst, k, count, src):
                b = (count - 1) % B
                act.wait_ge(mod_set, 6)
                act.wait_ge(turned, count)
                nc.scalar.activation(dst[:, b, :], src, ACT.Identity, bias=mod[:, k, 1, b:b + 1],
                                     scale=mod[:, k, 0, b:b + 1]).then_inc(hT_done, 1)

            def high_half(kind, b, h, count, v):
                act.wait_ge(proj_done, count + 1)
                if kind == "M":
                    nc.scalar.copy(Mhi[:, :, :], p_ps[:, 0:2 * P].rearrange("p (h d) -> p h d", h=2)).then_inc(hi_done, 1)
                else:
                    nc.scalar.copy(Ghi[:, b, h, :], p_ps[:, :]).then_inc(hi_done, 1)

            high_half("M", 0, 0, 1, 0)
            for b in range(B):
                modulate(h1T, 0, b + 1, t_ps[b][:, :])
                if b == 0:
                    high_half("G", 0, 0, 2, 1)
                    high_half("G", 0, 1, 3, 2)

            def exp(i, first, s):
                g = i * STEPS + s
                for h in range(2):
                    act.wait_ge(maxed, 2 * g + h + 1)
                    if not (first and s < 2):
                        act.wait_ge(p_turned, 2 * (g - 2) + h + 1)
                    nc.scalar.activation(prob[:, s % 2, h, :], s_ps[h][:, :], ACT.Exp, bias=negmax[:, s % 2, h:h + 1],
                                         accum_out=psumr[:, s % 2, h:h + 1]).then_inc(exped, 1)

            def read_turned(i, first, s):
                g, b, q = i * STEPS + s, s // QT, s % QT
                if q == 0 and not first:
                    act.wait_ge(pv_done, 2 * i + b - 1)
                for h in range(2):
                    act.wait_ge(p_turned, 2 * g + h + 1)
                    nc.scalar.copy(PT[:, b, h, :, q * P:(q + 1) * P],
                                   t_ps[h][:, :].rearrange("p (c q) -> p c q", c=QT)).then_inc(p_read, 1)

            exp(0, True, 0)

            def body(i, first, last):
                ahead, behind = projections(i, last)
                for s in range(STEPS):
                    if s < STEPS - 1:
                        exp(i, first, s + 1)
                    elif not last:
                        exp(i + 1, False, 0)
                    if s in ahead and ahead[s][0] == "G":
                        high_half(*ahead[s])
                    read_turned(i, first, s)
                    if s in behind:
                        high_half(*behind[s])

            rounds(act, body)

            for b in range(B):
                modulate(h2T, 1, 2 + b + 1, y_ps[b][:, :])

            def exp2(t):
                act.wait_ge(sub2_done, t + 1)
                nc.scalar.activation(e2[:, t % NE, :, :], e2[:, t % NE, :, :], ACT.Exp).then_inc(exp2_done, 1)

            exp2(0)
            for t in range(NT):
                if t + 1 < NT:
                    exp2(t + 1)
                act.wait_ge(t2_done, t + 1)
                if t >= 2:
                    act.wait_ge(out2_done, t - 1)
                nc.scalar.copy(PT2[:, t % 2, :, :], t_ps[t % 2][:, :].rearrange("p (c q) -> p c q", c=4)).then_inc(t2_read, 1)
            nc.scalar.activation(warm[:, 1:2], half[:, 0:1], ACT.Gelu)

            for b in range(B):
                modulate(h3T, 2, 4 + b + 1, y_ps[b][:, :])
                for c in range(FFC):
                    k = b * FFC + c
                    act.wait_ge(gate_ps, k + 1)
                    if k >= 2:
                        act.wait_ge(hid_done, k - 1)
                    nc.scalar.activation(gate[:, k % 2, :], s_ps[k % 2][:, :], ACT.Gelu,
                                         bias=cols[:, R_FB1 + FFC + c:R_FB1 + FFC + c + 1]).then_inc(gate_read, 1)
            for b in range(B):
                act.wait_ge(turned, 6 + b + 1)
                nc.scalar.copy(tT[:, b, :], y_ps[b][:, :]).then_inc(hT_done, 1)
                for c in range(FFC):
                    k = b * FFC + c
                    act.wait_ge(eh_ps, k + 1)
                    nc.scalar.activation(ehid[:, b, c, :], s_ps[k % 2][:, :], ACT.Relu,
                                         bias=cols[:, R_EB1 + c:R_EB1 + c + 1]).then_inc(eh_done, 1)

        @block.vector
        def _(dve):
            def statistics(k, t0, nt, src, c):
                for q in range(nt):
                    nc.vector.bn_stats(stats[:, t0 + q, :], src[:, t0 + q, :]).then_inc(stat_done, 1)
                for q in range(nt):
                    dve.wait_ge(stat_done, c + q + 1)
                    nc.vector.bn_aggr(meanvar[:, k, t0 + q, :], stats[:, t0 + q, :]).then_inc(aggr_done, 1)

            def apply_norm(k, t0, nt, src, dst, c):
                dve.wait_ge(rstd_done, c + 1)
                for t in range(t0, t0 + nt):
                    nc.vector.tensor_scalar(dst[:, t, :], src[:, t, :], meanvar[:, k, t, 0:1], rstd[:, k, t:t + 1],
                                            ALU.subtract, ALU.mult).then_inc(normed, 1)

            def batch_statistics(k, b, src):
                statistics(k, b * QT, QT, src, QT * (2 * k + b))

            def batch_apply(k, b, src, dst):
                apply_norm(k, b * QT, QT, src, dst, 2 * k + b)

            def read_projection(kind, b, h, count, v):
                if kind == "W":
                    dve.wait_ge(proj_done, count + 1)
                    nc.vector.tensor_scalar(wqT[:, :], p_ps[:, 0:P], SCALE, None, ALU.mult)
                    nc.vector.tensor_copy(wkT[0:DH, 0, :], p_ps[0:DH, P:2 * P])
                    nc.vector.tensor_copy(wkT[DH:P, 1, :], p_ps[DH:P, P:2 * P]).then_inc(proj_read, 1)
                elif kind == "M":
                    dve.wait_ge(hi_done, v + 1)
                    nc.vector.tensor_tensor(Mlo[:, :, :], p_ps[:, 0:2 * P].rearrange("p (h d) -> p h d", h=2),
                                            Mhi[:, :, :].bitcast(F32), ALU.subtract).then_inc(proj_read, 1)
                elif kind == "G":
                    dve.wait_ge(hi_done, v + 1)
                    nc.vector.tensor_tensor(Glo[:, b, h, :], p_ps[:, :], Ghi[:, b, h, :].bitcast(F32),
                                            ALU.subtract).then_inc(proj_read, 1)
                else:
                    dve.wait_ge(proj_done, count + 1)
                    nc.vector.tensor_copy(V[:, b, :, :], p_ps[:, :].rearrange("p (c d) -> p c d", c=QT)).then_inc(proj_read, 1)

            def read_prep(e):
                dve.wait_ge(c_ps, PREP_ORDER.index(e) + 1)
                four = o_ps[:, :].rearrange("p (c d) -> p c d", c=4)
                if e == "ctx":
                    nc.vector.tensor_copy(ctxT[:, :], o_ps[:, 0:B * CTX]).then_inc(c_read, 1)
                elif e in ("wq0", "wq1"):
                    c = 4 * int(e[2])
                    nc.vector.tensor_copy(wq2T[:, c:c + 4, :], four).then_inc(c_read, 1)
                elif e in ("K", "V"):
                    dst = bdK if e == "K" else bdV
                    dve.wait_ge(zero_set, 3)
                    v = o_ps[:, :].rearrange("p (c b k) -> p c b k", c=PAIRS, b=B)
                    nc.vector.tensor_copy(dst[0:DH, :, :, 0, :], v[0:DH])
                    nc.vector.tensor_copy(dst[DH:P, :, :, 1, :], v[DH:P]).then_inc(c_read, 1)
                elif e in ("A0", "A1"):
                    c = 4 * int(e[1])
                    nc.vector.tensor_scalar(A2[:, :, c:c + 4, :], o_ps[:, :].rearrange("p (c b k) -> p b c k", c=4, b=B),
                                            SCALE, None, ALU.mult).then_inc(c_read, 1)
                else:
                    nc.vector.tensor_copy(B2[:, int(e[1]), :, :], four).then_inc(c_read, 1)

            def row_max(i, s):
                g = i * STEPS + s
                for h in range(2):
                    dve.wait_ge(scored, 2 * g + h + 1)
                    nc.vector.tensor_reduce(negmax[:, s % 2, h:h + 1], s_ps[h][:, :], AX_X, ALU.max, negate=True).then_inc(maxed, 1)

            def normalise(i, s):
                g = i * STEPS + s
                for h in range(2):
                    dve.wait_ge(exped, 2 * g + h + 1)
                    nc.vector.reciprocal(rsum[:, s % 2, h:h + 1], psumr[:, s % 2, h:h + 1]).then_inc(summed, 1)
                for h in range(2):
                    dve.wait_ge(summed, 2 * g + h + 1)
                    nc.vector.tensor_scalar(prob[:, s % 2, h, :], prob[:, s % 2, h, :], rsum[:, s % 2, h:h + 1], None,
                                            ALU.mult).then_inc(probs_ready, 1)

            def read_o(u):
                dve.wait_ge(pv_done, u)
                nc.vector.tensor_copy(OT[:, :], o_ps[:, :]).then_inc(o_read, 1)

            def split_h1(b):
                dve.wait_ge(hT_done, b + 1)
                nc.vector.tensor_copy(h1hi[:, b, :], h1T[:, b, :]).then_inc(h1_split, 1)
                dve.wait_ge(h1_split, 2 * b + 1)
                nc.vector.tensor_tensor(h1lo[:, b, :], h1T[:, b, :], h1hi[:, b, :].bitcast(F32), ALU.subtract).then_inc(h1_split, 1)

            for b in range(B):
                dve.wait_ge(x_in[b], 16)
                batch_statistics(0, b, x)
            batch_apply(0, 0, x, xn)
            dve.wait_ge(normed, QT)
            batch_statistics(1, 0, xn)
            dve.wait_ge(cols_ps, 1)
            nc.vector.tensor_copy(cols[:, :], bank[6][:, 0:ROWS]).then_inc(cols_set, 1)
            batch_apply(0, 1, x, xn)
            batch_apply(1, 0, xn, n)
            dve.wait_ge(zero_set, 1)
            read_projection("W", 0, 0, 0, 0)
            dve.wait_ge(normed, QT * 2)
            batch_statistics(1, 1, xn)
            read_projection("M", 0, 0, 1, 0)
            dve.wait_ge(cols_set, 1)
            dve.wait_ge(mod_ps, 1)
            for k in range(3):
                for j in range(2):
                    col = cols[:, 2 + 2 * k + j:3 + 2 * k + j]
                    nc.vector.tensor_scalar(mod[:, k, j, :], bank[3][:, 4 * k + 2 * j:4 * k + 2 * j + 2], col,
                                            1.0 - j, ALU.add, ALU.add).then_inc(mod_set, 1)
            split_h1(0)
            batch_apply(1, 1, xn, n)
            read_projection("G", 0, 0, 2, 1)
            read_projection("G", 0, 1, 3, 2)
            row_max(0, 0)
            normalise(0, 0)
            split_h1(1)

            def body(i, first, last):
                ahead, behind = projections(i, last)
                for s in range(STEPS):
                    if s < STEPS - 1:
                        row_max(i, s + 1)
                    elif not last:
                        row_max(i + 1, 0)
                    for e in prep_of(first, s, 0):
                        read_prep(e)
                    if s in ahead:
                        read_projection(*ahead[s])
                    for e in prep_of(first, s, 1):
                        read_prep(e)
                    if s < STEPS - 1:
                        normalise(i, s + 1)
                    elif not last:
                        normalise(i + 1, 0)
                    for e in prep_of(first, s, 2):
                        read_prep(e)
                    if s in behind:
                        read_projection(*behind[s])
                    if s % QT == QT - 1 and not (first and s < QT):
                        u = 2 * i + s // QT
                        if not (first and s // QT <= 1):
                            dve.wait_ge(y_added, u - 1)
                        read_o(u)

            rounds(dve, body)
            dve.wait_ge(y_added, 2 * PAIRS - 1)
            read_o(2 * PAIRS)

            for b in range(B):
                dve.wait_ge(y_added, 2 * PAIRS - 1 + b)
                t = slice(b * QT, (b + 1) * QT)
                nc.vector.tensor_tensor(r1[:, t, :], y_ps[b][:, :].rearrange("p (q d) -> p q d", q=QT), xn[:, t, :],
                                        ALU.add).then_inc(r1_done, 1)
                dve.wait_ge(r1_done, b + 1)
                batch_statistics(2, b, r1)
            for b in range(B):
                batch_apply(2, b, r1, n)

            def scores2(t):
                dve.wait_ge(sc2_done, t + 1)
                sc = s_ps[t % 2][:, :].rearrange("p (h k) -> p h k", h=H)
                nc.vector.tensor_reduce(m2[:, t % NE, :], sc, AX_X, ALU.max).then_inc(max2_done, 1)
                dve.wait_ge(max2_done, t + 1)
                if t >= NE:
                    dve.wait_ge(t2_done, t - NE + 1)
                nc.vector.tensor_tensor(e2[:, t % NE, :, :], sc, m2[:, t % NE, :].to_broadcast([P, H, CTX]),
                                        ALU.subtract).then_inc(sub2_done, 1)

            def sums2(t):
                dve.wait_ge(exp2_done, t + 1)
                nc.vector.tensor_reduce(s2[:, t % NE, :], e2[:, t % NE, :, :], AX_X, ALU.add).then_inc(sum2_done, 1)
                dve.wait_ge(sum2_done, t + 1)
                nc.vector.reciprocal(i2[:, t % NE, :], s2[:, t % NE, :]).then_inc(inv2_done, 1)

            def join2(t):
                dve.wait_ge(out2_done, t + 1)
                dve.wait_ge(r1b_done, t // QT + 1)
                nc.vector.tensor_tensor(r2[:, t, :], bank[6 + t % 2][:, 0:D], r1b[:, t, :], ALU.add).then_inc(r2_done, 1)

            scores2(0)
            for t in range(NT):
                if t + 1 < NT:
                    scores2(t + 1)
                sums2(t)
                if t >= 2:
                    join2(t - 2)
                if t == QT + 1:
                    dve.wait_ge(r2_done, QT)
                    batch_statistics(3, 0, r2)
                if t == QT + 2:
                    batch_apply(3, 0, r2, n)
            join2(NT - 2)
            join2(NT - 1)
            dve.wait_ge(r2_done, NT)
            batch_statistics(3, 1, r2)

            def hidden(b, c):
                k = b * FFC + c
                dve.wait_ge(lin_ps, k + 1)
                dve.wait_ge(gate_read, k + 1)
                nc.vector.scalar_tensor_tensor(out=hid[:, b, c, :], in0=t_ps[k % 2][:, :],
                                               scalar=cols[:, R_FB1 + c:R_FB1 + c + 1], in1=gate[:, k % 2, :],
                                               op0=ALU.add, op1=ALU.mult).then_inc(hid_done, 1)

            def join3(b):
                t = slice(b * QT, (b + 1) * QT)
                dve.wait_ge(ff_ps, b + 1)
                dve.wait_ge(r2b_done, b + 1)
                nc.vector.tensor_tensor(r3[:, t, :], bank[6 + b][:, :].rearrange("p (q d) -> p q d", q=QT), r2b[:, t, :],
                                        ALU.add).then_inc(r3_done, 1)
                dve.wait_ge(r3_done, b + 1)
                batch_statistics(4, b, r3)

            hidden(0, 0)
            batch_apply(3, 1, r2, n)
            for c in range(1, FFC):
                hidden(0, c)
            join3(0)
            hidden(1, 0)
            batch_apply(4, 0, r3, tgt)
            for c in range(1, FFC):
                hidden(1, c)
            join3(1)
            batch_apply(4, 1, r3, tgt)

            def expert_sum(m):
                t = slice(2 * m, 2 * m + 2)
                ps = e_bank(m)[:, 0:2 * D].rearrange("p (q d) -> p q d", q=2)
                dve.wait_ge(e_ps, m + 1)
                dve.wait_ge(tgtb_done, m // 2 + 1)
                nc.vector.tensor_tensor(z[:, t, :], ps, tgtb[:, t, :], ALU.add).then_inc(z_done, 1)
                dve.wait_ge(z_done, m + 1)
                statistics(5, 2 * m, 2, z, QT * 2 * 5 + 2 * m)

            def expert_norm(m):
                t = slice(2 * m, 2 * m + 2)
                apply_norm(5, 2 * m, 2, z, zn, 2 * 5 + m)
                dve.wait_ge(normed, QT * 2 * 5 + 2 * (m + 1))
                nc.vector.tensor_tensor(zn[:, t, :], zn[:, t, :], spread[:, V_GAMMA:V_GAMMA + 1, :].to_broadcast([P, 2, D]),
                                        ALU.mult).then_inc(zg_done, 1)
                dve.wait_ge(zg_done, m + 1)
                dve.wait_ge(r3b_done, m // 2 + 1)
                nc.vector.tensor_tensor(zn[:, t, :], zn[:, t, :], r1[:, t, :], ALU.add).then_inc(res_done, 1)

            for m in range(2 * B):
                expert_sum(m)
                if m % 2:
                    expert_norm(m - 1)
                    expert_norm(m)

        @block.tensor
        def _(pe):
            mm = nc.tensor.matmul

            def exact(dst, lhi, llo, rhi, rlo):
                mm(dst, lhi, rhi, start=True, stop=False)
                mm(dst, lhi, rlo, start=False, stop=False)
                return mm(dst, llo, rhi, start=False, stop=True)

            def turn(src, b, dst):
                for q in range(QT):
                    last = nc.tensor.transpose(dst[:, q * P:(q + 1) * P], src[:, b * QT + q, :], ident[:, :])
                last.then_inc(turned, 1)

            def project(kind, b, h, count, v, i):
                if not (isinstance(count, int) and count == 0):
                    pe.wait_ge(proj_read, count)
                if kind == "W":
                    pe.wait_ge(stage_in, 32 * (i + 2))
                    for m in range(2):
                        last = nc.tensor.transpose(p_ps[:, m * P:(m + 1) * P], stage[:, m, :], ident[:, :])
                elif kind == "M":
                    last = mm(p_ps[:, 0:2 * P], wqT[:, :], wkT[:, :, :], start=True, stop=True)
                elif kind == "G":
                    last = exact(p_ps[:, :], Mhi[:, h, :], Mlo[:, h, :], h1hi[:, b, :], h1lo[:, b, :])
                else:
                    for c in range(QT):
                        last = mm(p_ps[:, c * P:(c + 1) * P], h1T[:, b, c * P:(c + 1) * P], wv[:, ds(i * P, P)],
                                  start=True, stop=True)
                last.then_inc(proj_done, 1)

            def prepare(e):
                c_before = PREP_ORDER.index(e)
                if c_before:
                    pe.wait_ge(c_read, c_before)
                if e == "ctx":
                    pe.wait_ge(ctx_in, 16)
                    last = nc.tensor.transpose(o_ps[:, 0:B * CTX], ctxt[:, :], ident[0:B * CTX, 0:B * CTX])
                elif e in ("wq0", "wq1"):
                    pe.wait_ge(wq2_in, 16)
                    for c in range(4):
                        w = (4 * int(e[2]) + c) * P
                        last = nc.tensor.transpose(o_ps[:, c * P:(c + 1) * P], wq2[:, w:w + P], ident[:, :])
                elif e in ("K", "V"):
                    w = wk2 if e == "K" else wv2
                    pe.wait_ge(wk2_in if e == "K" else wv2_in, 16)
                    for c in range(PAIRS):
                        last = mm(o_ps[:, c * B * CTX:(c + 1) * B * CTX], w[:, c * P:(c + 1) * P], ctxT[:, :],
                                  start=True, stop=True)
                elif e in ("A0", "A1"):
                    for c in range(4):
                        w = 4 * int(e[1]) + c
                        last = mm(o_ps[:, c * P:(c + 1) * P], wq2T[:, w, :], bdK[:, w, :, :, :], start=True, stop=True)
                else:
                    pe.wait_ge(wo2_in, 16)
                    for c in range(PAIRS):
                        last = mm(o_ps[(c % 2) * DH:(c % 2 + 1) * DH, (c // 2) * D:(c // 2 + 1) * D],
                                  bdV[:, c, int(e[1]), :, :], wo2[:, c, :], start=True, stop=True)
                last.then_inc(c_ps, 1)

            def scores(i, first, s):
                g, b, q = i * STEPS + s, s // QT, s % QT
                t = slice(q * P, (q + 1) * P)
                for h in range(2):
                    if not (first and s == 0):
                        pe.wait_ge(exped, 2 * (g - 1) + h + 1)
                    exact(s_ps[h][:, :], Ghi[:, b, h, t], Glo[:, b, h, t], h1hi[:, b, :], h1lo[:, b, :]).then_inc(scored, 1)

            def turn_probs(i, first, s):
                g = i * STEPS + s
                for h in range(2):
                    pe.wait_ge(probs_ready, 2 * g + h + 1)
                    if not (first and s == 0):
                        pe.wait_ge(p_read, 2 * (g - 1) + h + 1)
                    for c in range(QT):
                        last = nc.tensor.transpose(t_ps[h][:, c * P:(c + 1) * P], prob[:, s % 2, h, c * P:(c + 1) * P], ident[:, :])
                    last.then_inc(p_turned, 1)

            def times_v(b, c):
                for h in range(2):
                    last = mm(o_ps[h * DH:(h + 1) * DH, :], V[:, b, c, h * DH:(h + 1) * DH], PT[:, b, h, c, :],
                              start=(c == 0), stop=(c == QT - 1), skip_group_check=True)
                if c == QT - 1:
                    last.then_inc(pv_done, 1)

            def add_y(b, pair, u):
                pe.wait_ge(o_read, u + 1)
                for q in range(QT):
                    last = mm(y_ps[b][:, q * P:(q + 1) * P], OT[:, q * P:(q + 1) * P],
                              wo[:, pair, :] if isinstance(pair, int) else wo[:, ds(pair, 1), :],
                              start=False, stop=False, skip_group_check=True)
                last.then_inc(y_added, 1)

            pe.wait_ge(ident_done, 1)
            pe.wait_ge(rows_in, 16 * 6)
            nc.tensor.transpose(bank[6][:, 0:ROWS], rows[:, :], ident[0:ROWS, 0:ROWS]).then_inc(cols_ps, 1)
            pe.wait_ge(stage_in, 32)
            for m in range(2):
                last = nc.tensor.transpose(p_ps[:, m * P:(m + 1) * P], stage[:, m, :], ident[:, :])
            last.then_inc(proj_done, 1)
            pe.wait_ge(bo1_in, 16)
            for b in range(B):
                mm(y_ps[b][:, :], ones[:, :], bo1row[:, :, :], start=True, stop=False, skip_group_check=True)
            pe.wait_ge(cols_set, 1)
            pe.wait_ge(nw_in, 48)
            for k in range(3):
                for j in range(2):
                    last = mm(bank[3][:, 4 * k + 2 * j:4 * k + 2 * j + 2], nw[:, k, j * D:(j + 1) * D],
                              cols[:, R_COND:R_COND + 2], start=True, stop=True)
            last.then_inc(mod_ps, 1)
            project("M", 0, 0, 1, 0, 0)
            pe.wait_ge(normed, QT * 3)
            turn(n, 0, t_ps[0])
            pe.wait_ge(h1_split, 2)
            project("G", 0, 0, 2, 1, 0)
            pe.wait_ge(normed, QT * 4)
            turn(n, 1, t_ps[1])
            project("G", 0, 1, 3, 2, 0)
            pe.wait_ge(proj_read, 4)
            scores(0, True, 0)
            pe.wait_ge(h1_split, 4)
            pe.wait_ge(wv_in, 16)

            def body(i, first, last):
                ahead, behind = projections(i, last)
                for s in range(STEPS):
                    b, q = s // QT, s % QT
                    if s == QT - 1:
                        pe.wait_ge(proj_read, ahead[1][3] + 1)
                    if s < STEPS - 1:
                        scores(i, first, s + 1)
                    elif not last:
                        pe.wait_ge(proj_read, ahead[5][3] + 1)
                        scores(i + 1, False, 0)
                    for e in prep_of(first, s, 0):
                        prepare(e)
                    if s in ahead:
                        project(*ahead[s], i)
                    for e in prep_of(first, s, 1):
                        prepare(e)
                    turn_probs(i, first, s)
                    for e in prep_of(first, s, 2):
                        prepare(e)
                    if s in behind:
                        project(*behind[s], i)
                    u = 2 * i + b
                    if q == 0 and not (first and b == 0):
                        if first and b == 1:
                            pe.wait_ge(c_read, len(PREP_ORDER))
                        else:
                            if first is False and b == 0:
                                pe.wait_ge(wo_in, 16)
                            add_y(b, i - 1, u - 2)
                            pe.wait_ge(o_read, u - 1)
                        pe.wait_ge(p_read, 2 * QT * u)
                        if b == 0:
                            pe.wait_ge(proj_read, ahead[0][3])
                        else:
                            pe.wait_ge(proj_read, ahead[3][3] + 1)
                    if not (first and b == 0):
                        times_v(1 - b, q)

            rounds(pe, body)
            add_y(0, PAIRS - 1, 2 * PAIRS - 2)
            pe.wait_ge(p_read, 2 * QT * 2 * PAIRS)
            pe.wait_ge(proj_read, (PAIRS - 1) * PROJ_ROUND + PROJ_BEFORE + 4)
            for c in range(QT):
                times_v(1, c)
            add_y(1, PAIRS - 1, 2 * PAIRS - 1)

            for b in range(B):
                pe.wait_ge(normed, QT * (2 * 2 + b + 1))
                turn(n, b, y_ps[b])
                if b == 0:
                    pe.wait_ge(c_read, len(PREP_ORDER))

            def scores_2(t):
                if t >= 2:
                    pe.wait_ge(sub2_done, t - 1)
                pe.wait_ge(hT_done, 2 + t // QT + 1)
                mm(s_ps[t % 2][:, :], h2T[:, t // QT, (t % QT) * P:(t % QT + 1) * P], A2[:, t // QT, :, :],
                   start=True, stop=True).then_inc(sc2_done, 1)

            def turn_2(t):
                pe.wait_ge(nrm2_done, t + 1)
                if t >= 2:
                    pe.wait_ge(t2_read, t - 1)
                for c in range(4):
                    last = nc.tensor.transpose(t_ps[t % 2][:, c * P:(c + 1) * P], e2[:, t % NE, 4 * c:4 * c + 4, :], ident[:, :])
                last.then_inc(t2_done, 1)

            def out_2(t):
                pe.wait_ge(t2_read, t + 1)
                if t >= 2:
                    pe.wait_ge(r2_done, t - 1)
                for c in range(4):
                    last = mm(bank[6 + t % 2][:, 0:D], PT2[:, t % 2, c, :], B2[:, t // QT, c, :],
                              start=(c == 0), stop=(c == 3))
                last.then_inc(out2_done, 1)

            scores_2(0)
            scores_2(1)
            for t in range(NT):
                if t + 2 < NT:
                    scores_2(t + 2)
                turn_2(t)
                if t >= 1:
                    out_2(t - 1)
            pe.wait_ge(normed, QT * (2 * 3 + 1))
            turn(n, 0, y_ps[0])
            out_2(NT - 1)

            def up(b):
                pe.wait_ge(hT_done, 4 + b + 1)
                for c in range(FFC):
                    k = b * FFC + c
                    if k >= 2:
                        pe.wait_ge(gate_read, k - 1)
                    mm(s_ps[k % 2][:, :], fw1[:, DFF + c * P:DFF + (c + 1) * P], h3T[:, b, :], start=True, stop=True).then_inc(gate_ps, 1)
                    if k >= 2:
                        pe.wait_ge(hid_done, k - 1)
                    mm(t_ps[k % 2][:, :], fw1[:, c * P:(c + 1) * P], h3T[:, b, :], start=True, stop=True).then_inc(lin_ps, 1)

            def down(b, q, dst, w, hidden):
                for c in range(FFC):
                    last = mm(dst, hidden[:, b, c, q * P:(q + 1) * P], w[:, c, :],
                              start=(c == 0), stop=(c == FFC - 1))
                return last

            pe.wait_ge(ff_in, 32)
            for b in range(B):
                if b == 1:
                    pe.wait_ge(normed, QT * (2 * 3 + 2))
                    turn(n, 1, y_ps[1])
                up(b)
                pe.wait_ge(hid_done, FFC * (b + 1))
                pe.wait_ge(r2_done, NT)
                for q in range(QT):
                    last = down(b, q, bank[6 + b][:, q * P:(q + 1) * P], fw2, hid)
                last.then_inc(ff_ps, 1)
            pe.wait_ge(ew_in, 32)
            for b in range(B):
                pe.wait_ge(normed, QT * (2 * 4 + b + 1))
                turn(tgt, b, y_ps[b])
                pe.wait_ge(hT_done, 6 + b + 1)
                for c in range(FFC):
                    k = b * FFC + c
                    if k >= 2:
                        pe.wait_ge(eh_done, k - 1)
                    mm(s_ps[k % 2][:, :], ew1[:, c * P:(c + 1) * P], tT[:, b, :], start=True, stop=True).then_inc(eh_ps, 1)
                pe.wait_ge(eh_done, FFC * (b + 1))
                pe.wait_ge(r3_done, b + 1)
                for q in range(QT):
                    last = down(b, q, e_bank(2 * b + q // 2)[:, (q % 2) * P:(q % 2 + 1) * P], ew2, ehid)
                    if q % 2:
                        last.then_inc(e_ps, 1)


_X = "L0_xcond_"
_INS = (["x", "cond_1024", "ctx_1024"] + [_X + f"attn{k}_{w}" for k in (1, 2) for w in ("wq", "wk", "wv", "wo", "bo")]
        + [_X + w for w in ("ff_w1", "ff_b1", "ff_w2", "ff_b2")] + [_X + f"norm{k}_{w}" for k in (1, 2, 3) for w in "wb"]
        + ["L0_ffn_" + w for w in ("w1", "b1", "w2", "b2", "gamma", "beta")])


def kernel(**inputs):
    import numpy as _np
    import concourse.bacc as _bacc
    from concourse import mybir as _mybir
    from concourse.bass_utils import run_bass_kernel_spmd as _run

    nc = _bacc.Bacc("TRN2", target_bir_lowering=False, num_devices=1)
    arrays, args = {}, {}
    for name in _INS:
        v = _np.ascontiguousarray(inputs[name])
        arrays[f"in_{name}"] = v
        args[name] = nc.dram_tensor(f"in_{name}", v.shape, _mybir.dt.from_np(v.dtype), kind="ExternalInput").ap()
    out = nc.dram_tensor("out_0", (B, S, D), F32, kind="ExternalOutput").ap()
    residual_block(nc, args, out)
    r = _run(nc, [arrays], core_ids=[0])
    return r.results[0]["out_0"]
```

```python
from contextlib import ExitStack

import concourse.bass as bass
from concourse import mybir

F32 = mybir.dt.float32
F32R = mybir.dt.float32r
ALU = mybir.AluOpType
ACT = mybir.ActivationFunctionType
AX_X = mybir.AxisListType.X
ds = bass.ds

P = 128
B, S, D, H, DH, CTX = 2, 512, 128, 16, 64, 32
QT = S // P
NT = B * QT
PAIRS = H // 2
STEPS = B * QT
DFF = 4 * D
FFC = DFF // P
SCALE = 1.0 / 8.0
EPS = 1e-5
NLN = 6
WARM = (24, 8, 12, 4, 12)

R_COND, R_N1, R_N2, R_N3, R_FB1, R_EB1 = 0, 2, 4, 6, 8, 16
COLS = 20
V_FB2, V_BO2, V_EB2, V_GAMMA, V_BETA = range(5)


def residual_block(nc, a, out):
    x_d = a["x"].rearrange("b (t p) d -> p (b t) d", p=P)
    out_d = out.rearrange("b (t p) d -> p (b t) d", p=P)
    pre = "L0_xcond_"
    wqT_d, wkT_d, wv_d = (a[v] for v in ("wq1T", "wk1T", pre + "attn1_wv"))
    wo_d = a[pre + "attn1_wo"].rearrange("(c p) d -> p c d", p=P)
    wo2_d = a[pre + "attn2_wo"].rearrange("(c p) d -> p c d", p=P)
    fw2_d = a[pre + "ff_w2"].rearrange("(c p) d -> p c d", p=P)
    ew1_d = a["L0_ffn_w1"][0]
    ew2_d = a["L0_ffn_w2"][0].rearrange("(c p) d -> p c d", p=P)

    with ExitStack() as ctx:
        def sb(name, *shape, dt=F32):
            return ctx.enter_context(nc.sbuf_tensor(name, list(shape), dt))

        def sem(name):
            return ctx.enter_context(nc.semaphore(name))

        x = sb("x", P, NT, D)
        xn = sb("xn", P, NT, D)
        n = sb("n", P, NT, D)
        r1 = sb("r1", P, NT, D)
        r2b = sb("r2b", P, NT, D)
        stats = sb("stats", P, NT, 6)
        meanvar = sb("meanvar", P, NLN, NT, 2)
        rstd = sb("rstd", P, NLN, NT)
        half = sb("half", P, QT)
        warm = sb("warm", P, 2)
        ident = sb("ident", P, P)
        ones = sb("ones", 1, P)
        cols = sb("cols", P, COLS)
        spread = sb("spread", P, 5, D)
        bo1row = sb("bo1row", 1, QT, D)
        nw = sb("nw", P, 3, 2 * D)
        mod = sb("mod", P, 3, 2, B)
        h1T = sb("h1T", P, B, S)
        h1hi = sb("h1hi", P, B, S, dt=F32R)
        h1lo = sb("h1lo", P, B, S, dt=F32R)
        wv = sb("wv", P, H * DH)
        wo = sb("wo", P, PAIRS, D)
        wqT = sb("wqT", P, P)
        wkT = sb("wkT", P, 2, P)
        Mhi = sb("Mhi", P, 2, P, dt=F32R)
        Mlo = sb("Mlo", P, 2, P, dt=F32R)
        Ghi = sb("Ghi", P, B, 2, S, dt=F32R)
        Glo = sb("Glo", P, B, 2, S, dt=F32R)
        wvhi = sb("wvhi", P, H * DH, dt=F32R)
        wvlo = sb("wvlo", P, H * DH, dt=F32R)
        V = sb("V", P, B, QT, 4 * DH)
        prob = sb("prob", P, 2, 2, S)
        negmax = sb("negmax", P, 2, 2)
        psumr = sb("psumr", P, 2, 2)
        rsum = sb("rsum", P, 2, 2)
        PT = sb("PT", P, B, 2, QT, S)
        OT = sb("OT", P, S)
        ctxT = sb("ctxT", P, B * CTX)
        wk2 = sb("wk2", P, H * DH)
        wv2 = sb("wv2", P, H * DH)
        wo2 = sb("wo2", P, PAIRS, D)
        wq2T = sb("wq2T", P, PAIRS, P)
        bdK = sb("bdK", P, PAIRS, B, 2, CTX)
        bdV = sb("bdV", P, PAIRS, B, 2, CTX)
        A2 = sb("A2", P, B, PAIRS, 2 * CTX)
        B2 = sb("B2", P, B, 4, D)
        m2 = sb("m2", P, NT, H)
        s2 = sb("s2", P, NT, H)
        i2 = sb("i2", P, NT, H)
        PT2 = sb("PT2", P, 2, 4, P)
        fw1 = sb("fw1", P, 2 * DFF)
        fw1hi = sb("fw1hi", P, 2 * DFF, dt=F32R)
        fw1lo = sb("fw1lo", P, 2 * DFF, dt=F32R)
        fw2 = sb("fw2", P, FFC, D)
        ew1 = sb("ew1", P, DFF)
        ew1hi = sb("ew1hi", P, DFF, dt=F32R)
        ew1lo = sb("ew1lo", P, DFF, dt=F32R)
        ew2 = sb("ew2", P, FFC, D)

        r1b = wk2[:, :].rearrange("p (t d) -> p t d", d=D)
        r2 = wv2[:, :].rearrange("p (t d) -> p t d", d=D)
        r3 = wo2[:, :, :]
        tgt = wq2T[:, :, :]
        tgtb = bdK[:, :, :, :, :].rearrange("p t b h k -> p t (b h k)")
        z = bdV[:, :, :, :, :].rearrange("p t b h k -> p t (b h k)")
        e2 = [PT[:, b, 1, q, :].rearrange("p (h k) -> p h k", h=H)
              for b in range(B) for q in range(QT)]
        h2T, h3T = prob[:, 0, :, :], prob[:, 1, :, :]
        gate = V[:, :, :, :].rearrange("p b c d -> p b (c d)")
        uphi, uplo = h1hi, h1lo
        zn = wv[:, :].rearrange("p (t d) -> p t d", d=D)
        hid = PT[:, :, 0, :, :]
        ehid = PT[:, :, 1, :, :]

        bank = [ctx.enter_context(nc.psum_tensor(f"bank{k}", [P, 512], F32)) for k in range(8)]
        y_ps = bank[0:2]
        s_ps = bank[2:4]
        t_ps = bank[4:6]
        o_ps = bank[6]
        p_ps = bank[7]

        x_in = [sem("x_in0"), sem("x_in1"), sem("x_in2")]
        cols_in, nw0_in, nw_in, spread_in = sem("cols_in"), sem("nw0_in"), sem("nw_in"), sem("spread_in")
        pair_in, wv_in, wo_in = sem("pair_in"), sem("wv_in"), sem("wo_in")
        ctx_in, wq2_in, wk2_in, wv2_in, wo2_in = (sem(v) for v in ("ctx_in", "wq2_in", "wk2_in", "wv2_in", "wo2_in"))
        bo1_in, fw1_in, fw2_in, ew1_in, ew2_in = (sem(v) for v in ("bo1_in", "fw1_in", "fw2_in", "ew1_in", "ew2_in"))
        stored = sem("stored")
        const_set, ident_done, zero_set = sem("const_set"), sem("ident_done"), sem("zero_set")
        mod_ps, mod_set, w_hi, w_split = sem("mod_ps"), sem("mod_set"), sem("w_hi"), sem("w_split")
        stat_done, aggr_done, eps_done = sem("stat_done"), sem("aggr_done"), sem("eps_done")
        rstd_done, normed = sem("rstd_done"), sem("normed")
        turned, hT_done, h1_split = sem("turned"), sem("hT_done"), sem("h1_split")
        proj_done, hi_done, proj_read = sem("proj_done"), sem("hi_done"), sem("proj_read")
        scored, maxed, exped = sem("scored"), sem("maxed"), sem("exped")
        summed, probs_ready = sem("summed"), sem("probs_ready")
        p_turned, p_read = sem("p_turned"), sem("p_read")
        pv_done, o_read, y_added = sem("pv_done"), sem("o_read"), sem("y_added")
        c_ps, c_read = sem("c_ps"), sem("c_read")
        sc2_done, max2_done, sub2_done = sem("sc2_done"), sem("max2_done"), sem("sub2_done")
        exp2_done, sum2_done, inv2_done, nrm2_done = sem("exp2_done"), sem("sum2_done"), sem("inv2_done"), sem("nrm2_done")
        t2_done, t2_read, out2_done = sem("t2_done"), sem("t2_read"), sem("out2_done")
        r1_done, r1b_done, r2_done, r2b_done = sem("r1_done"), sem("r1b_done"), sem("r2_done"), sem("r2b_done")
        r3_done, r3b_done, tgtb_done, z_done, zg_done = sem("r3_done"), sem("r3b_done"), sem("tgtb_done"), sem("z_done"), sem("zg_done")
        xr_done = sem("xr_done")
        res_done = sem("res_done")
        up_hi, up_split = sem("up_hi"), sem("up_split")
        up_ps, gate_read, hid_done = sem("up_ps"), sem("gate_read"), sem("hid_done")
        ff_ps, eh_ps, eh_done, e_ps = sem("ff_ps"), sem("eh_ps"), sem("eh_done"), sem("e_ps")

        HI_BEFORE, HI_ROUND = 3, 5
        PREP = {1: "K", 2: "V", 3: "A0", 4: "A1", 5: "B0", 6: "B1"}
        PREP_ORDER = list(PREP.values())

        def projections(i, odd, first, last):
            order = [(0, "G", 1, 0), (1, "G", 1, 1), (2, "M", 0, 0), (4, "G", 0, 0), (5, "G", 0, 1)]
            if last:
                order = order[0:2]
            elif odd:
                order += [(6, "V", 0, 0)]
            else:
                order = order[0:3] + [(3, "V", 0, 0)] * first + [(3, "V", 0, 1)] + order[3:] + [(6, "V", 1, 0), (7, "V", 1, 1)]
            c = 3 if first else 7 * i + (5 if odd else 4)
            v = i * HI_ROUND + HI_BEFORE
            steps, read = {}, {}
            for j, (s, kind, b, h) in enumerate(order):
                late = first and (kind, b, h) == ("G", 1, 0)
                ps = o_ps if first and (kind, b, h) in (("G", 1, 1), ("V", 0, 1)) else p_ps
                steps.setdefault(s + late, []).append((kind, b, h, c + j, v, ps))
                read[kind, b, h] = c + j + 1
                v = v + (kind != "V")
            return steps, read

        NORMS = ([(0, 0, 2), (0, 2, 2), (1, 0, 2), (1, 2, 2), (0, QT, QT), (1, QT, QT), (2, 0, QT), (2, QT, 2), (2, QT + 2, 2)]
                 + [(k, t, 2) for k in range(3, NLN) for t in range(0, NT, 2)])

        def norm_at(k, t0):
            i = [v[:2] for v in NORMS].index((k, t0))
            return i, sum(v[2] for v in NORMS[:i])

        def tokens(g):
            return slice((g % 2) * 2 * P, (g % 2 + 1) * 2 * P)

        LAST = PAIRS - 1

        def rounds(eng, body):
            body(0, False, True, False)
            with eng.Fori(0, (PAIRS - 2) // 2) as j:
                body(2 * j + 1, True, False, False)
                body(2 * j + 2, False, False, False)
            body(PAIRS - 1, True, False, True)

        block = ctx.enter_context(nc.Block())

        @block.sync
        def _(sp):
            def load_pair(rows):
                sp.dma_start(wqT[:, :], wqT_d[rows(0), :]).then_inc(pair_in, 16)
                sp.dma_start(wkT[0:DH, 0, :], wkT_d[rows(1), :]).then_inc(pair_in, 16)
                sp.dma_start(wkT[DH:P, 1, :], wkT_d[rows(2), :]).then_inc(pair_in, 16)

            def pair_rows(i):
                return lambda m: (ds(i * P, P), ds(i * P, DH), ds(i * P + DH, DH))[m]

            sp.dma_start(x[:, 0:2, :], x_d[:, 0:2, :]).then_inc(x_in[0], 16)
            sp.dma_start(x[:, 2:QT, :], x_d[:, 2:QT, :]).then_inc(x_in[1], 16)
            load_pair(pair_rows(0))
            sp.dma_start(x[:, QT:NT, :], x_d[:, QT:NT, :]).then_inc(x_in[2], 16)
            for k in range(1, 3):
                sp.dma_start(nw[:, k, :], a[pre + f"norm{k + 1}_w"]).then_inc(nw_in, 16)
            sp.dma_start(wv[:, :], wv_d).then_inc(wv_in, 16)
            sp.dma_start(ctxT[:, :], a["ctxT"]).then_inc(ctx_in, 16)
            sp.dma_start(wk2[:, :], a[pre + "attn2_wk"]).then_inc(wk2_in, 16)
            sp.dma_start(wv2[:, :], a[pre + "attn2_wv"]).then_inc(wv2_in, 16)
            sp.wait_ge(proj_done, 1)
            load_pair(pair_rows(1))
            sp.dma_start(wq2T[:, :, :], a["wq2T"].rearrange("(c p) d -> p c d", p=P)).then_inc(wq2_in, 16)
            sp.dma_start(wo2[:, :, :], wo2_d).then_inc(wo2_in, 16)
            sp.dma_start(wo[:, :, :], wo_d).then_inc(wo_in, 16)
            sp.dma_start(bo1row[:, :, :], a[pre + "attn1_bo"].rearrange("(a c d) -> a c d", a=1, c=1).to_broadcast([1, QT, D])).then_inc(bo1_in, 16)
            for k, v in ((V_FB2, a[pre + "ff_b2"]), (V_BO2, a[pre + "attn2_bo"]), (V_EB2, a["L0_ffn_b2"][0]),
                         (V_GAMMA, a["L0_ffn_gamma"]), (V_BETA, a["L0_ffn_beta"])):
                sp.dma_start(spread[:, k, :], v.rearrange("(a d) -> a d", a=1).to_broadcast([P, D])).then_inc(spread_in, 16)
            sp.dma_start(fw1[:, :], a[pre + "ff_w1"]).then_inc(fw1_in, 16)
            sp.dma_start(ew1[:, :], ew1_d).then_inc(ew1_in, 16)
            sp.dma_start(fw2[:, :, :], fw2_d).then_inc(fw2_in, 16)
            sp.dma_start(ew2[:, :, :], ew2_d).then_inc(ew2_in, 16)
            with sp.Fori(1, PAIRS - 1) as i:
                sp.wait_ge(proj_done, 7 * (i - 1) + 5 + 3)
                load_pair(pair_rows(i + 1))
            for m in range(2 * B):
                sp.wait_ge(res_done, 2 * (m + 1))
                sp.dma_start(out_d[:, 2 * m:2 * m + 2, :], zn[:, 2 * m:2 * m + 2, :]).then_inc(stored, 16)
            sp.wait_ge(stored, 16 * 2 * B)

        @block.gpsimd
        def _(pool):
            nc.gpsimd.memset(ident[:, :], 0.0).then_inc(const_set, 1)
            nc.gpsimd.memset(half[:, :], -0.5).then_inc(const_set, 1)
            nc.gpsimd.memset(ones[:, :], 1.0).then_inc(const_set, 1)
            pool.wait_ge(const_set, 3)
            nc.gpsimd.affine_select(out=ident[:, :], in_=ident[:, :], compare_op=ALU.not_equal, fill=1.0,
                                    base=0, pattern=[[-1, P]], channel_multiplier=1).then_inc(ident_done, 1)
            pool.wait_ge(ident_done, 1)
            nc.gpsimd.memset(wkT[DH:P, 0, :], 0.0).then_inc(zero_set, 1)
            pool.wait_ge(zero_set, 1)
            nc.gpsimd.memset(wkT[0:DH, 1, :], 0.0).then_inc(zero_set, 1)
            pool.wait_ge(zero_set, 2)

            def power(k, t0, nt):
                i, tiles = norm_at(k, t0)
                r = rstd[:, k, t0:t0 + nt]
                pool.wait_ge(aggr_done, tiles + nt)
                nc.gpsimd.tensor_scalar(r, meanvar[:, k, t0:t0 + nt, 1], EPS, None, ALU.add).then_inc(eps_done, 1)
                pool.wait_ge(eps_done, i + 1)
                nc.gpsimd.tensor_tensor(r, r, half[:, 0:nt], ALU.pow).then_inc(rstd_done, 1)

            def power3(g):
                power(3, 2 * g, 2)

            def power4(g):
                power(4, 2 * g, 2)

            def power5(g):
                power(5, 2 * g, 2)

            def group(t, g):
                return t[:, 2 * g:2 * g + 2, :]

            def group_vector(k):
                return spread[:, k:k + 1, :].to_broadcast([P, 2, D])

            def batch(t, b):
                return t[:, b * QT:(b + 1) * QT, :]

            def split_weights(w, hi, lo, landed, before):
                pool.wait_ge(landed, 16)
                for c in range(0, w.shape[1], 2 * P):
                    before += 1
                    nc.gpsimd.tensor_copy(hi[:, c:c + 2 * P], w[:, c:c + 2 * P]).then_inc(w_hi, 1)
                    pool.wait_ge(w_hi, before)
                    nc.gpsimd.tensor_tensor(lo[:, c:c + 2 * P], w[:, c:c + 2 * P], hi[:, c:c + 2 * P].bitcast(F32),
                                            ALU.subtract).then_inc(w_split, 1)

            def vector(k):
                return spread[:, k:k + 1, :].to_broadcast([P, QT, D])

            for k, t, nt in NORMS[0:6]:
                power(k, t, nt)
            split_weights(wv, wvhi, wvlo, wv_in, 0)
            nc.gpsimd.memset(bdK[:, :, :, :, :], 0.0).then_inc(zero_set, 1)
            nc.gpsimd.memset(bdV[:, :, :, :, :], 0.0).then_inc(zero_set, 1)
            pool.wait_ge(spread_in, 16 * 5)
            for b in range(B):
                nc.gpsimd.tensor_tensor(batch(r2b, b), batch(x, b), vector(V_FB2), ALU.add).then_inc(xr_done, 1)

            split_weights(fw1, fw1hi, fw1lo, fw1_in, H * DH // (2 * P))
            split_weights(ew1, ew1hi, ew1lo, ew1_in, (H * DH + 2 * DFF) // (2 * P))

            def add_bias2(b):
                pool.wait_ge(r1_done, 2 * b + 1)
                nc.gpsimd.tensor_tensor(batch(r1b, b), batch(r1, b), vector(V_BO2), ALU.add).then_inc(r1b_done, 1)

            def normalise2(t):
                pool.wait_ge(inv2_done, t + 1)
                nc.gpsimd.tensor_tensor(e2[t], e2[t],
                                        i2[:, t, :].to_broadcast([P, H, CTX]), ALU.mult).then_inc(nrm2_done, 1)

            def add_r2(g):
                pool.wait_ge(xr_done, g // 2 + 1)
                pool.wait_ge(r2_done, 2 * (g + 1))
                nc.gpsimd.tensor_tensor(group(r2b, g), group(r2b, g), group(r2, g), ALU.add).then_inc(r2b_done, 1)

            def add_eb2(g):
                pool.wait_ge(normed, norm_at(4, 2 * g)[1] + 2)
                nc.gpsimd.tensor_tensor(group(tgtb, g), group(tgt, g), group_vector(V_EB2), ALU.add).then_inc(tgtb_done, 1)

            def add_beta(g):
                pool.wait_ge(r3_done, g + 1)
                nc.gpsimd.tensor_tensor(group(r1, g), group(r3, g), group_vector(V_BETA), ALU.add).then_inc(r3b_done, 1)

            power(2, 0, QT)
            add_bias2(0)
            normalise2(0)
            normalise2(1)
            power(2, QT, 2)
            normalise2(2)
            power(2, QT + 2, 2)
            normalise2(3)
            add_bias2(1)
            power3(0)
            normalise2(4)
            normalise2(5)
            add_r2(0)
            power3(1)
            normalise2(6)
            normalise2(7)
            add_r2(1)
            power3(2)
            add_r2(2)
            power3(3)
            power4(0)
            add_beta(0)
            add_eb2(0)
            power4(1)
            add_beta(1)
            power4(2)
            add_r2(3)
            power4(3)
            add_beta(2)
            power5(0)
            add_eb2(1)
            add_eb2(2)
            add_beta(3)
            power5(1)
            add_eb2(3)
            power5(2)
            power5(3)

        @block.scalar
        def _(act):
            act.dma_start(cols[:, :], a["cols"]).then_inc(cols_in, 16)
            act.dma_start(nw[:, 0, :], a[pre + "norm1_w"]).then_inc(nw0_in, 16)
            act.wait_ge(const_set, 3)
            nc.scalar.activation(warm[:, 0:1], half[:, 0:1], ACT.Exp)

            def modulate(dst, k, b, count, src):
                act.wait_ge(mod_set, 2 * (k + 1))
                act.wait_ge(turned, count)
                nc.scalar.activation(dst, src, ACT.Identity, bias=mod[:, k, 1, b:b + 1],
                                     scale=mod[:, k, 0, b:b + 1]).then_inc(hT_done, 1)

            def high_half(kind, b, h, count, v, p_ps=p_ps):
                act.wait_ge(proj_done, count + 1)
                if kind == "M":
                    nc.scalar.mul(Mhi[:, :, :], p_ps[:, 0:2 * P].rearrange("p (h d) -> p h d", h=2), SCALE).then_inc(hi_done, 1)
                else:
                    nc.scalar.copy(Ghi[:, b, h, :], p_ps[:, :]).then_inc(hi_done, 1)

            high_half("M", 0, 0, 0, 0)
            modulate(h1T[:, 0, :], 0, 0, 1, t_ps[0][:, :])
            high_half("G", 0, 0, 1, 1)
            high_half("G", 0, 1, 2, 2, o_ps)

            def exp(i, first, s, heads=range(2)):
                g = i * STEPS + s
                for h in heads:
                    act.wait_ge(maxed, 2 * g + h + 1)
                    if not (first and s < 2):
                        act.wait_ge(p_turned, 2 * (g - 2) + h + 1)
                    nc.scalar.activation(prob[:, s % 2, h, :], s_ps[h][:, :], ACT.Exp, bias=negmax[:, s % 2, h:h + 1],
                                         accum_out=psumr[:, s % 2, h:h + 1]).then_inc(exped, 1)

            def read_turned(i, first, s, heads=range(2)):
                g, b, q = i * STEPS + s, s // QT, s % QT
                if q == 0 and not first:
                    act.wait_ge(pv_done, 2 * i + b - 1)
                for h in heads:
                    act.wait_ge(p_turned, 2 * g + h + 1)
                    nc.scalar.copy(PT[:, b, h, :, q * P:(q + 1) * P],
                                   t_ps[h][:, :].rearrange("p (c q) -> p c q", c=QT)).then_inc(p_read, 1)

            exp(0, True, 0)

            def body(i, odd, first, last):
                ahead, _ = projections(i, odd, first, last)
                for s in range(QT if last else STEPS):
                    if s < STEPS - 1:
                        exp(i, first, s + 1)
                    elif not last:
                        exp(i + 1, False, 0)
                    if first and s == 0:
                        modulate(h1T[:, 1, :], 0, 1, 2, y_ps[1][:, :])
                    for job in ahead.get(s, []):
                        if job[0] != "V":
                            high_half(*job)
                    read_turned(i, first, s)

            rounds(act, body)

            def modulate2(m):
                if m == 0:
                    act.wait_ge(p_turned, 2 * (LAST * STEPS + 7))
                    modulate(h2T[:, 0, :], 1, 0, 3, y_ps[0][:, :])
                else:
                    modulate(h2T[:, 1, (m - 1) * 2 * P:m * 2 * P], 1, 1, 3 + m, y_ps[m % 2][:, 0:2 * P])

            def exp2(t):
                act.wait_ge(sub2_done, t + 1)
                nc.scalar.activation(e2[t], e2[t], ACT.Exp).then_inc(exp2_done, 1)

            def read_turned2(t):
                act.wait_ge(t2_done, t + 1)
                if t >= 2:
                    act.wait_ge(out2_done, t - 1)
                nc.scalar.copy(PT2[:, t % 2, :, :], t_ps[t % 2][:, :].rearrange("p (c q) -> p c q", c=4)).then_inc(t2_read, 1)

            def load_gelu():
                nc.scalar.activation(warm[:, 1:2], half[:, 0:1], ACT.Gelu)

            def modulate3(g):
                modulate(h3T[:, g // 2, tokens(g)], 2, g // 2, 6 + g, y_ps[g % 2][:, 0:2 * P])

            def high_h3(g):
                act.wait_ge(hT_done, 6 + g)
                nc.scalar.activation(uphi[:, g // 2, tokens(g)], y_ps[g % 2][:, 0:2 * P], ACT.Identity,
                                     bias=mod[:, 2, 1, g // 2:g // 2 + 1],
                                     scale=mod[:, 2, 0, g // 2:g // 2 + 1]).then_inc(up_hi, 1)

            def gelu(k):
                c = k % FFC
                act.wait_ge(up_ps, k + 1)
                nc.scalar.activation(gate[:, k % 2, 0:2 * P], s_ps[k % 2][:, 0:2 * P], ACT.Gelu,
                                     bias=cols[:, R_FB1 + FFC + c:R_FB1 + FFC + c + 1]).then_inc(gate_read, 1)

            def high_tgt(g):
                act.wait_ge(turned, 10 + g)
                nc.scalar.copy(uphi[:, g // 2, tokens(g)], y_ps[g % 2][:, 0:2 * P]).then_inc(up_hi, 1)

            def relu(k):
                g, c = k // FFC, k % FFC
                act.wait_ge(eh_ps, k + 1)
                nc.scalar.activation(ehid[:, g // 2, c, tokens(g)], s_ps[k % 2][:, 0:2 * P], ACT.Relu,
                                     bias=cols[:, R_EB1 + c:R_EB1 + c + 1]).then_inc(eh_done, 1)

            exp(LAST, False, 5)
            exp(LAST, False, 6, heads=(0,))
            read_turned(LAST, False, 4)
            read_turned(LAST, False, 5, heads=(0,))
            exp(LAST, False, 6, heads=(1,))
            exp(LAST, False, 7, heads=(0,))
            read_turned(LAST, False, 5, heads=(1,))
            read_turned(LAST, False, 6, heads=(0,))
            modulate2(0)
            exp(LAST, False, 7, heads=(1,))
            read_turned(LAST, False, 6, heads=(1,))
            read_turned(LAST, False, 7, heads=(0,))
            exp2(0)
            read_turned(LAST, False, 7, heads=(1,))
            exp2(1)
            read_turned2(0)
            exp2(2)
            read_turned2(1)
            exp2(3)
            modulate2(1)
            exp2(4)
            read_turned2(2)
            modulate2(2)
            read_turned2(3)
            exp2(5)
            read_turned2(4)
            modulate3(0)
            high_h3(0)
            exp2(6)
            read_turned2(5)
            exp2(7)
            load_gelu()
            gelu(0)
            gelu(1)
            modulate3(1)
            read_turned2(6)
            high_h3(1)
            gelu(2)
            gelu(3)
            read_turned2(7)
            for k in range(4, 7):
                gelu(k)
            modulate3(2)
            high_h3(2)
            for k in range(7, 10):
                gelu(k)
            modulate3(3)
            high_h3(3)
            for k in range(10, 14):
                gelu(k)
            high_tgt(0)
            gelu(14)
            gelu(15)
            high_tgt(1)
            for k in range(0, 6):
                relu(k)
            high_tgt(2)
            for k in range(6, 9):
                relu(k)
            high_tgt(3)
            for k in range(9, 16):
                relu(k)

        @block.vector
        def _(dve):
            def statistics(k, t0, nt, src):
                before = norm_at(k, t0)[1]
                for q in range(nt):
                    nc.vector.bn_stats(stats[:, t0 + q, :], src[:, t0 + q, :]).then_inc(stat_done, 1)
                for q in range(nt):
                    dve.wait_ge(stat_done, before + q + 1)
                    nc.vector.bn_aggr(meanvar[:, k, t0 + q, :], stats[:, t0 + q, :]).then_inc(aggr_done, 1)

            def apply_norm(k, t0, nt, src, dst):
                dve.wait_ge(rstd_done, norm_at(k, t0)[0] + 1)
                for t in range(t0, t0 + nt):
                    nc.vector.tensor_scalar(dst[:, t, :], src[:, t, :], meanvar[:, k, t, 0:1], rstd[:, k, t:t + 1],
                                            ALU.subtract, ALU.mult).then_inc(normed, 1)

            def read_projection(kind, b, h, count, v, p_ps=p_ps):
                if kind == "M":
                    dve.wait_ge(hi_done, v + 1)
                    nc.vector.scalar_tensor_tensor(out=Mlo[:, :, :].rearrange("p h d -> p (h d)"), in0=p_ps[:, 0:2 * P], scalar=SCALE,
                                                   in1=Mhi[:, :, :].rearrange("p h d -> p (h d)").bitcast(F32),
                                                   op0=ALU.mult, op1=ALU.subtract).then_inc(proj_read, 1)
                elif kind == "G":
                    dve.wait_ge(hi_done, v + 1)
                    nc.vector.tensor_tensor(Glo[:, b, h, :], p_ps[:, :], Ghi[:, b, h, :].bitcast(F32),
                                            ALU.subtract).then_inc(proj_read, 1)
                else:
                    dve.wait_ge(proj_done, count + 1)
                    nc.vector.tensor_copy(V[:, b, 2 * h:2 * h + 2, :], p_ps[:, :].rearrange("p (c d) -> p c d", c=2)).then_inc(proj_read, 1)

            def read_prep(e):
                m = PREP_ORDER.index(e)
                ps = y_ps[m % 2]
                dve.wait_ge(c_ps, m + 1)
                if e in ("K", "V"):
                    dst = bdK if e == "K" else bdV
                    dve.wait_ge(zero_set, 4)
                    v = ps[:, :].rearrange("p (c b k) -> p c b k", c=PAIRS, b=B)
                    nc.vector.tensor_copy(dst[0:DH, :, :, 0, :], v[0:DH])
                    nc.vector.tensor_copy(dst[DH:P, :, :, 1, :], v[DH:P]).then_inc(c_read, 1)
                elif e in ("A0", "A1"):
                    c = 4 * int(e[1])
                    nc.vector.tensor_scalar(A2[:, :, c:c + 4, :], ps[:, :].rearrange("p (c b k) -> p b c k", c=4, b=B),
                                            SCALE, None, ALU.mult).then_inc(c_read, 1)
                else:
                    nc.vector.tensor_copy(B2[:, int(e[1]), :, :], ps[:, :].rearrange("p (c d) -> p c d", c=4)).then_inc(c_read, 1)

            def row_max(i, s, heads=range(2)):
                g = i * STEPS + s
                for h in heads:
                    dve.wait_ge(scored, 2 * g + h + 1)
                    nc.vector.tensor_reduce(negmax[:, s % 2, h:h + 1], s_ps[h][:, :], AX_X, ALU.max, negate=True).then_inc(maxed, 1)

            def normalise(i, s, heads=range(2)):
                g = i * STEPS + s
                for h in heads:
                    dve.wait_ge(exped, 2 * g + h + 1)
                    nc.vector.reciprocal(rsum[:, s % 2, h:h + 1], psumr[:, s % 2, h:h + 1]).then_inc(summed, 1)
                    dve.wait_ge(summed, 2 * g + h + 1)
                    nc.vector.tensor_scalar(prob[:, s % 2, h, :], prob[:, s % 2, h, :], rsum[:, s % 2, h:h + 1], None,
                                            ALU.mult).then_inc(probs_ready, 1)

            def read_o(u):
                dve.wait_ge(pv_done, u)
                if not (isinstance(u, int) and u == 1):
                    dve.wait_ge(y_added, u - 1)
                nc.vector.tensor_copy(OT[:, :], o_ps[:, :]).then_inc(o_read, 1)

            def split_h1(b):
                dve.wait_ge(hT_done, b + 1)
                nc.vector.tensor_copy(h1hi[:, b, :], h1T[:, b, :]).then_inc(h1_split, 1)
                dve.wait_ge(h1_split, 2 * b + 1)
                nc.vector.tensor_tensor(h1lo[:, b, :], h1T[:, b, :], h1hi[:, b, :].bitcast(F32), ALU.subtract).then_inc(h1_split, 1)

            def modulation(k):
                for j in range(2):
                    nc.vector.tensor_scalar(mod[:, k, j, :], bank[3][:, 4 * k + 2 * j:4 * k + 2 * j + 2],
                                            cols[:, 2 + 2 * k + j:3 + 2 * k + j], 1.0 - j, ALU.add, ALU.add).then_inc(mod_set, 1)

            for t in (0, 2):
                dve.wait_ge(x_in[t // 2], 16)
                statistics(0, t, 2, x)
            for t in (0, 2):
                apply_norm(0, t, 2, x, xn)
                dve.wait_ge(normed, t + 2)
                statistics(1, t, 2, xn)
            for t in (0, 2):
                apply_norm(1, t, 2, xn, n)
            dve.wait_ge(cols_in, 16)
            dve.wait_ge(mod_ps, 1)
            modulation(0)
            read_projection("M", 0, 0, 0, 0)
            split_h1(0)
            dve.wait_ge(x_in[2], 16)
            statistics(0, QT, QT, x)
            dve.wait_ge(mod_ps, 2)
            modulation(1)
            modulation(2)
            read_projection("G", 0, 0, 1, 1)
            read_projection("G", 0, 1, 2, 2, o_ps)
            apply_norm(0, QT, QT, x, xn)
            row_max(0, 0)
            dve.wait_ge(normed, QT * 3)
            statistics(1, QT, QT, xn)
            normalise(0, 0)

            def body(i, odd, first, last):
                ahead, _ = projections(i, odd, first, last)
                for s in range(QT if last else STEPS):
                    if s < STEPS - 1:
                        row_max(i, s + 1)
                        if first and s == 0:
                            apply_norm(1, QT, QT, xn, n)
                    elif not last:
                        row_max(i + 1, 0)
                    if s < STEPS - 1:
                        normalise(i, s + 1)
                    elif not last:
                        normalise(i + 1, 0)
                    for job in ahead.get(s, []):
                        read_projection(*job)
                    if first and s == 0:
                        split_h1(1)
                    if first and s in PREP:
                        read_prep(PREP[s])
                    if s % QT == QT - 1 and not (first and s < QT) and not last:
                        read_o(2 * i + s // QT)

            rounds(dve, body)

            def join1(t0, nt):
                b, t, c = t0 // QT, slice(t0, t0 + nt), (t0 % QT) * P
                dve.wait_ge(y_added, 2 * PAIRS - 1 + b)
                nc.vector.tensor_tensor(r1[:, t, :], y_ps[b][:, c:c + nt * P].rearrange("p (q d) -> p q d", q=nt), xn[:, t, :],
                                        ALU.add).then_inc(r1_done, 1)
                dve.wait_ge(r1_done, (0, QT, QT + 2).index(t0) + 1)

            def scores2(t):
                dve.wait_ge(sc2_done, t + 1)
                sc = s_ps[t % 2][:, :].rearrange("p (h k) -> p h k", h=H)
                nc.vector.tensor_reduce(m2[:, t, :], sc, AX_X, ALU.max).then_inc(max2_done, 1)
                dve.wait_ge(max2_done, t + 1)
                if t % QT == 0:
                    dve.wait_ge(pv_done, 2 * PAIRS - 1 + t // QT)
                nc.vector.tensor_tensor(e2[t], sc, m2[:, t, :].to_broadcast([P, H, CTX]),
                                        ALU.subtract).then_inc(sub2_done, 1)

            def sums2(t):
                dve.wait_ge(exp2_done, t + 1)
                nc.vector.tensor_reduce(s2[:, t, :], e2[t], AX_X, ALU.add).then_inc(sum2_done, 1)
                dve.wait_ge(sum2_done, t + 1)
                nc.vector.reciprocal(i2[:, t, :], s2[:, t, :]).then_inc(inv2_done, 1)

            def join2(t):
                dve.wait_ge(out2_done, t + 1)
                dve.wait_ge(r1b_done, t // QT + 1)
                nc.vector.tensor_tensor(r2[:, t, :], bank[6 + t % 2][:, 0:D], r1b[:, t, :], ALU.add).then_inc(r2_done, 1)

            def statistics3(g):
                dve.wait_ge(r2_done, 2 * (g + 1))
                statistics(3, 2 * g, 2, r2)

            def apply3(g):
                apply_norm(3, 2 * g, 2, r2, n)

            def low_h3(g):
                dve.wait_ge(up_hi, g + 1)
                t = tokens(g)
                nc.vector.tensor_tensor(uplo[:, g // 2, t], h3T[:, g // 2, t], uphi[:, g // 2, t].bitcast(F32),
                                        ALU.subtract).then_inc(up_split, 1)

            def hidden(k):
                g, c = k // FFC, k % FFC
                dve.wait_ge(gate_read, k + 1)
                nc.vector.scalar_tensor_tensor(out=hid[:, g // 2, c, tokens(g)], in0=s_ps[k % 2][:, 2 * P:4 * P],
                                               scalar=cols[:, R_FB1 + c:R_FB1 + c + 1], in1=gate[:, k % 2, 0:2 * P],
                                               op0=ALU.add, op1=ALU.mult).then_inc(hid_done, 1)

            def join3(g):
                t = slice(2 * g, 2 * g + 2)
                dve.wait_ge(ff_ps, g + 1)
                dve.wait_ge(r2b_done, g + 1)
                nc.vector.tensor_tensor(r3[:, t, :], bank[6 + g % 2][:, 0:2 * P].rearrange("p (q d) -> p q d", q=2), r2b[:, t, :],
                                        ALU.add).then_inc(r3_done, 1)

            def statistics4(g):
                dve.wait_ge(r3_done, g + 1)
                statistics(4, 2 * g, 2, r3)

            def apply4(g):
                apply_norm(4, 2 * g, 2, r3, tgt)

            def low_tgt(g):
                dve.wait_ge(up_hi, NT // 2 + g + 1)
                t = tokens(g)
                nc.vector.tensor_tensor(uplo[:, g // 2, t], y_ps[g % 2][:, 0:2 * P], uphi[:, g // 2, t].bitcast(F32),
                                        ALU.subtract).then_inc(up_split, 1)

            def expert_sum(g):
                t = slice(2 * g, 2 * g + 2)
                dve.wait_ge(e_ps, g + 1)
                dve.wait_ge(tgtb_done, g + 1)
                nc.vector.tensor_tensor(z[:, t, :], t_ps[g % 2][:, 0:2 * P].rearrange("p (q d) -> p q d", q=2), tgtb[:, t, :],
                                        ALU.add).then_inc(z_done, 1)
                dve.wait_ge(z_done, g + 1)
                statistics(5, 2 * g, 2, z)

            def times_gamma(g):
                for t in (2 * g, 2 * g + 1):
                    dve.wait_ge(aggr_done, norm_at(5, 2 * g)[1] + 2)
                    nc.vector.scalar_tensor_tensor(out=zn[:, t, :], in0=z[:, t, :], scalar=meanvar[:, 5, t, 0:1],
                                                   in1=spread[:, V_GAMMA, :], op0=ALU.subtract, op1=ALU.mult).then_inc(zg_done, 1)

            def finish(g):
                dve.wait_ge(rstd_done, norm_at(5, 2 * g)[0] + 1)
                dve.wait_ge(r3b_done, g + 1)
                dve.wait_ge(zg_done, 2 * (g + 1))
                for t in (2 * g, 2 * g + 1):
                    nc.vector.scalar_tensor_tensor(out=zn[:, t, :], in0=zn[:, t, :], scalar=rstd[:, 5, t:t + 1],
                                                   in1=r1[:, t, :], op0=ALU.mult, op1=ALU.add).then_inc(res_done, 1)

            read_o(2 * PAIRS - 2)
            row_max(LAST, 5)
            normalise(LAST, 5, heads=(0,))
            read_o(2 * PAIRS - 1)
            normalise(LAST, 5, heads=(1,))
            row_max(LAST, 6, heads=(0,))
            join1(0, QT)
            statistics(2, 0, QT, r1)
            row_max(LAST, 6, heads=(1,))
            normalise(LAST, 6, heads=(0,))
            row_max(LAST, 7, heads=(0,))
            apply_norm(2, 0, QT, r1, n)
            normalise(LAST, 6, heads=(1,))
            row_max(LAST, 7, heads=(1,))
            normalise(LAST, 7)
            scores2(0)
            scores2(1)
            sums2(0)
            sums2(1)
            read_o(2 * PAIRS)
            scores2(2)
            join1(QT, 2)
            statistics(2, QT, 2, r1)
            join1(QT + 2, 2)
            scores2(3)
            apply_norm(2, QT, 2, r1, n)
            join2(0)
            sums2(2)
            statistics(2, QT + 2, 2, r1)
            join2(1)
            sums2(3)
            scores2(4)
            apply_norm(2, QT + 2, 2, r1, n)
            statistics3(0)
            scores2(5)
            sums2(4)
            join2(2)
            sums2(5)
            apply3(0)
            join2(3)
            scores2(6)
            statistics3(1)
            scores2(7)
            low_h3(0)
            sums2(6)
            apply3(1)
            sums2(7)
            hidden(0)
            hidden(1)
            join2(4)
            join2(5)
            statistics3(2)
            low_h3(1)
            hidden(2)
            hidden(3)
            apply3(2)
            join2(6)
            hidden(4)
            join2(7)
            statistics3(3)
            hidden(5)
            hidden(6)
            low_h3(2)
            apply3(3)
            hidden(7)
            join3(0)
            hidden(8)
            statistics4(0)
            hidden(9)
            low_h3(3)
            hidden(10)
            apply4(0)
            hidden(11)
            join3(1)
            statistics4(1)
            hidden(12)
            hidden(13)
            apply4(1)
            low_tgt(0)
            hidden(14)
            hidden(15)
            join3(2)
            statistics4(2)
            low_tgt(1)
            apply4(2)
            join3(3)
            statistics4(3)
            low_tgt(2)
            apply4(3)
            expert_sum(0)
            low_tgt(3)
            times_gamma(0)
            expert_sum(1)
            times_gamma(1)
            finish(0)
            finish(1)
            expert_sum(2)
            times_gamma(2)
            expert_sum(3)
            finish(2)
            times_gamma(3)
            finish(3)

        @block.tensor
        def _(pe):
            mm = nc.tensor.matmul

            def exact(dst, lhi, llo, rhi, rlo):
                mm(dst, lhi, rhi, start=True, stop=False)
                mm(dst, lhi, rlo, start=False, stop=False)
                return mm(dst, llo, rhi, start=False, stop=True)

            def turn(src, t0, nt, dst):
                for q in range(nt):
                    last = nc.tensor.transpose(dst[:, q * P:(q + 1) * P], src[:, t0 + q, :], ident[:, :])
                last.then_inc(turned, 1)

            def turn_normed(k, t0, nt, src, dst):
                pe.wait_ge(normed, norm_at(k, t0)[1] + nt)
                turn(src, t0, nt, dst)

            def project(kind, b, h, count, v, p_ps=p_ps, i=0, odd=False):
                pe.wait_ge(proj_read, count if p_ps is bank[7] else count - 1)
                if kind == "M":
                    pe.wait_ge(pair_in, 48 * (i + 2))
                    last = mm(p_ps[:, 0:2 * P], wqT[:, :], wkT[:, :, :], start=True, stop=True)
                elif kind == "G":
                    last = exact(p_ps[:, :], Mhi[:, h, :], Mlo[:, h, :], h1hi[:, b, :], h1lo[:, b, :])
                else:
                    w = ds((i + odd) * P, 2 * P)
                    for m in range(2):
                        c = slice((2 * h + m) * P, (2 * h + m + 1) * P)
                        last = exact(p_ps[:, m * 2 * P:(m + 1) * 2 * P], h1hi[:, b, c], h1lo[:, b, c], wvhi[:, w], wvlo[:, w])
                last.then_inc(proj_done, 1)

            def prepare(e):
                m = PREP_ORDER.index(e)
                ps = y_ps[m % 2]
                if m >= 2:
                    pe.wait_ge(c_read, m - 1)
                if e in ("K", "V"):
                    w = wk2 if e == "K" else wv2
                    pe.wait_ge(ctx_in, 16)
                    pe.wait_ge(hT_done, 2)
                    pe.wait_ge(wk2_in if e == "K" else wv2_in, 16)
                    for c in range(PAIRS):
                        last = mm(ps[:, c * B * CTX:(c + 1) * B * CTX], w[:, c * P:(c + 1) * P], ctxT[:, :],
                                  start=True, stop=True)
                elif e in ("A0", "A1"):
                    pe.wait_ge(wq2_in, 16)
                    for c in range(4):
                        w = 4 * int(e[1]) + c
                        last = mm(ps[:, c * P:(c + 1) * P], wq2T[:, w, :], bdK[:, w, :, :, :], start=True, stop=True)
                else:
                    pe.wait_ge(wo2_in, 16)
                    for c in range(PAIRS):
                        last = mm(ps[(c % 2) * DH:(c % 2 + 1) * DH, (c // 2) * D:(c // 2 + 1) * D],
                                  bdV[:, c, int(e[1]), :, :], wo2[:, c, :], start=True, stop=True)
                last.then_inc(c_ps, 1)

            def start_y():
                pe.wait_ge(c_read, len(PREP_ORDER))
                pe.wait_ge(bo1_in, 16)
                pe.wait_ge(wo_in, 16)
                for b in range(B):
                    mm(y_ps[b][:, :], ones[:, :], bo1row[:, :, :], start=True, stop=False, skip_group_check=True)

            def scores(i, first, s, heads=range(2)):
                g, b, q = i * STEPS + s, s // QT, s % QT
                t = slice(q * P, (q + 1) * P)
                for h in heads:
                    if not (first and s == 0):
                        pe.wait_ge(exped, 2 * (g - 1) + h + 1)
                    exact(s_ps[h][:, :], Ghi[:, b, h, t], Glo[:, b, h, t], h1hi[:, b, :], h1lo[:, b, :]).then_inc(scored, 1)

            def turn_probs(i, first, s, heads=range(2)):
                g = i * STEPS + s
                for h in heads:
                    pe.wait_ge(probs_ready, 2 * g + h + 1)
                    if not (first and s == 0):
                        pe.wait_ge(p_read, 2 * (g - 1) + h + 1)
                    for c in range(QT):
                        last = nc.tensor.transpose(t_ps[h][:, c * P:(c + 1) * P], prob[:, s % 2, h, c * P:(c + 1) * P], ident[:, :])
                    last.then_inc(p_turned, 1)

            def times_v(b, c, odd):
                for h in range(2):
                    d = (2 * odd + h) * DH
                    last = mm(o_ps[h * DH:(h + 1) * DH, :], V[:, b, c, d:d + DH], PT[:, b, h, c, :],
                              start=(c == 0), stop=(c == QT - 1), skip_group_check=True)
                if c == QT - 1:
                    last.then_inc(pv_done, 1)

            def add_y(b, pair, u):
                pe.wait_ge(o_read, u + 1)
                for q in range(QT):
                    last = mm(y_ps[b][:, q * P:(q + 1) * P], OT[:, q * P:(q + 1) * P],
                              wo[:, pair, :] if isinstance(pair, int) else wo[:, ds(pair, 1), :],
                              start=False, stop=False, skip_group_check=True)
                last.then_inc(y_added, 1)

            def modulation(k):
                for j in range(2):
                    last = mm(bank[3][:, 4 * k + 2 * j:4 * k + 2 * j + 2], nw[:, k, j * D:(j + 1) * D],
                              cols[:, R_COND:R_COND + 2], start=True, stop=True)
                return last

            def keep_clock(count):
                for _ in range(count):
                    nc.tensor.transpose(y_ps[0][:, 0:P], ident[:, :], ident[:, :])

            pe.wait_ge(const_set, 3)
            pe.wait_ge(ident_done, 1)
            keep_clock(WARM[0])
            pe.wait_ge(cols_in, 16)
            pe.wait_ge(nw0_in, 16)
            modulation(0).then_inc(mod_ps, 1)
            keep_clock(WARM[1])
            pe.wait_ge(pair_in, 48)
            pe.wait_ge(zero_set, 2)
            mm(p_ps[:, 0:2 * P], wqT[:, :], wkT[:, :, :], start=True, stop=True).then_inc(proj_done, 1)
            pe.wait_ge(normed, QT * 2)
            turn(n, 0, QT, t_ps[0])
            pe.wait_ge(mod_set, 2)
            pe.wait_ge(nw_in, 32)
            modulation(1)
            modulation(2).then_inc(mod_ps, 1)
            keep_clock(WARM[2])
            pe.wait_ge(h1_split, 2)
            project("G", 0, 0, 1, 1)
            project("G", 0, 1, 2, 2, o_ps)
            keep_clock(WARM[3])
            pe.wait_ge(proj_read, 2)
            scores(0, True, 0, heads=(0,))
            pe.wait_ge(proj_read, 3)
            pe.wait_ge(mod_set, 6)
            scores(0, True, 0, heads=(1,))
            keep_clock(WARM[4])

            def body(i, odd, first, last):
                ahead, read = projections(i, odd, first, last)
                for s in range(QT if last else STEPS):
                    b, q = s // QT, s % QT
                    if s == QT - 1:
                        pe.wait_ge(proj_read, read["G", 1, 1])
                    if s < STEPS - 1:
                        scores(i, first, s + 1)
                    elif not last:
                        pe.wait_ge(proj_read, read["G", 0, 1])
                        scores(i + 1, False, 0)
                    for job in ahead.get(s, []):
                        if first and s == 1:
                            pe.wait_ge(h1_split, 4)
                        if first and s == 3:
                            pe.wait_ge(w_split, H * DH // (2 * P))
                        project(*job, i, odd)
                    if q == QT - 1 and odd:
                        add_y(b, i - 1, 2 * i + b - 2)
                    turn_probs(i, first, s)
                    if first and s == 0:
                        pe.wait_ge(normed, QT * 4)
                        turn(n, QT, QT, y_ps[1])
                    if first and s in PREP:
                        prepare(PREP[s])
                    u = 2 * i + b
                    if q == 0 and not odd and not first:
                        add_y(b, i - 1, u - 2)
                    if q == 0 and not (first and b == 0):
                        if not first:
                            pe.wait_ge(o_read, u - 1)
                        pe.wait_ge(p_read, 2 * QT * u)
                    if not (first and b == 0):
                        times_v(1 - b, q, odd if b == 1 else not odd)
                if first:
                    start_y()

            rounds(pe, body)

            def times_v_0(c):
                if c == 0:
                    pe.wait_ge(p_read, 2 * QT * (2 * PAIRS - 1))
                    pe.wait_ge(o_read, 2 * PAIRS - 2)
                times_v(0, c, True)

            def times_v_tile(q):
                pe.wait_ge(p_read, 2 * (QT * (2 * PAIRS - 1) + q + 1))
                pe.wait_ge(o_read, 2 * PAIRS - 1)
                for c in range(QT):
                    for h in range(2):
                        last = mm(o_ps[h * DH:(h + 1) * DH, q * P:(q + 1) * P], V[:, 1, c, (2 + h) * DH:(3 + h) * DH],
                                  PT[:, 1, h, c, q * P:(q + 1) * P], start=(c == 0), stop=(c == QT - 1),
                                  skip_group_check=True)
                if q == QT - 1:
                    last.then_inc(pv_done, 1)

            def turn_n2(m):
                if m == 0:
                    turn_normed(2, 0, QT, n, y_ps[0])
                elif m == 1:
                    pe.wait_ge(r1_done, 3)
                    turn_normed(2, QT, 2, n, y_ps[1])
                else:
                    pe.wait_ge(hT_done, 3)
                    turn_normed(2, QT + 2, 2, n, y_ps[0])

            def turn_n3(g):
                if g < 2:
                    pe.wait_ge(hT_done, 5 - g)
                else:
                    pe.wait_ge(up_hi, g - 1)
                turn_normed(3, 2 * g, 2, n, y_ps[g % 2])

            def turn_tgt(g):
                if g < 2:
                    pe.wait_ge(up_hi, g + 3)
                else:
                    pe.wait_ge(up_split, NT // 2 + g - 1)
                turn_normed(4, 2 * g, 2, tgt, y_ps[g % 2])

            def scores_2(t):
                if t < 2:
                    pe.wait_ge(exped, 2 * (PAIRS * STEPS - 1) + t + 1)
                else:
                    pe.wait_ge(sub2_done, t - 1)
                pe.wait_ge(hT_done, 3 if t < QT else 2 + t // 2)
                mm(s_ps[t % 2][:, :], h2T[:, t // QT, (t % QT) * P:(t % QT + 1) * P], A2[:, t // QT, :, :],
                   start=True, stop=True).then_inc(sc2_done, 1)

            def turn_2(t):
                pe.wait_ge(nrm2_done, t + 1)
                if t < 2:
                    pe.wait_ge(p_read, 2 * (PAIRS * STEPS - 1) + t + 1)
                else:
                    pe.wait_ge(t2_read, t - 1)
                for c in range(4):
                    last = nc.tensor.transpose(t_ps[t % 2][:, c * P:(c + 1) * P], e2[t][:, 4 * c:4 * c + 4, :], ident[:, :])
                last.then_inc(t2_done, 1)

            def out_2(t):
                pe.wait_ge(t2_read, t + 1)
                if t < 2:
                    pe.wait_ge(o_read, 2 * PAIRS)
                else:
                    pe.wait_ge(r2_done, t - 1)
                for c in range(4):
                    last = mm(bank[6 + t % 2][:, 0:D], PT2[:, t % 2, c, :], B2[:, t // QT, c, :],
                              start=(c == 0), stop=(c == 3))
                last.then_inc(out2_done, 1)

            def up(k):
                g, c = k // FFC, k % FFC
                if k == 0:
                    pe.wait_ge(w_split, (H * DH + 3 * DFF) // (2 * P))
                if k < 2:
                    pe.wait_ge(sub2_done, NT)
                else:
                    pe.wait_ge(hid_done, k - 1)
                pe.wait_ge(up_split, g + 1)
                t = tokens(g)
                for dst, w in ((s_ps[k % 2][:, 0:2 * P], slice(DFF + c * P, DFF + (c + 1) * P)),
                               (s_ps[k % 2][:, 2 * P:4 * P], slice(c * P, (c + 1) * P))):
                    last = exact(dst, fw1hi[:, w], fw1lo[:, w], uphi[:, g // 2, t], uplo[:, g // 2, t])
                last.then_inc(up_ps, 1)

            def expert_up(k):
                g, c = k // FFC, k % FFC
                if k < 2:
                    pe.wait_ge(hid_done, NT // 2 * FFC - 1 + k)
                else:
                    pe.wait_ge(eh_done, k - 1)
                pe.wait_ge(up_split, NT // 2 + g + 1)
                w, t = slice(c * P, (c + 1) * P), tokens(g)
                exact(s_ps[k % 2][:, 0:2 * P], ew1hi[:, w], ew1lo[:, w], uphi[:, g // 2, t], uplo[:, g // 2, t]).then_inc(eh_ps, 1)

            def down(t, dst, w, hidden, done):
                g, q = t // 2, t % QT
                for c in range(FFC):
                    if t % 2 == 0:
                        pe.wait_ge(done, FFC * g + c + 1)
                    last = mm(dst[:, (t % 2) * P:(t % 2 + 1) * P], hidden[:, g // 2, c, q * P:(q + 1) * P], w[:, c, :],
                              start=(c == 0), stop=(c == FFC - 1))
                return last

            def feed_down(t):
                g = t // 2
                if t == 0:
                    pe.wait_ge(fw2_in, 16)
                if g < 2:
                    pe.wait_ge(r2_done, NT)
                else:
                    pe.wait_ge(r3_done, g - 1)
                last = down(t, bank[6 + g % 2], fw2, hid, hid_done)
                if t % 2:
                    last.then_inc(ff_ps, 1)

            def expert_down(t):
                g = t // 2
                if t == 0:
                    pe.wait_ge(ew2_in, 16)
                if g < 2:
                    pe.wait_ge(t2_read, NT)
                else:
                    pe.wait_ge(z_done, g - 1)
                last = down(t, t_ps[g % 2], ew2, ehid, eh_done)
                if t % 2:
                    last.then_inc(e_ps, 1)

            scores(LAST, False, 5)
            for k in range(0, 3):
                times_v_0(k)
            add_y(1, PAIRS - 2, 2 * PAIRS - 3)
            times_v_0(3)
            scores(LAST, False, 6, heads=(0,))
            add_y(0, PAIRS - 1, 2 * PAIRS - 2)
            turn_probs(LAST, False, 4, heads=(0,))
            scores(LAST, False, 6, heads=(1,))
            turn_probs(LAST, False, 4, heads=(1,))
            scores(LAST, False, 7, heads=(0,))
            turn_probs(LAST, False, 5)
            times_v_tile(0)
            turn_probs(LAST, False, 6, heads=(0,))
            scores(LAST, False, 7, heads=(1,))
            turn_n2(0)
            turn_probs(LAST, False, 6, heads=(1,))
            times_v_tile(1)
            scores_2(0)
            scores_2(1)
            turn_probs(LAST, False, 7)
            times_v_tile(2)
            scores_2(2)
            times_v_tile(3)
            scores_2(3)
            add_y(1, PAIRS - 1, 2 * PAIRS - 1)
            turn_2(0)
            turn_2(1)
            out_2(0)
            out_2(1)
            turn_n2(1)
            scores_2(4)
            turn_2(2)
            scores_2(5)
            turn_2(3)
            turn_n2(2)
            out_2(2)
            out_2(3)
            scores_2(6)
            scores_2(7)
            turn_2(4)
            turn_n3(0)
            turn_2(5)
            out_2(4)
            out_2(5)
            up(0)
            up(1)
            turn_n3(1)
            turn_2(6)
            up(2)
            up(3)
            turn_2(7)
            out_2(6)
            up(4)
            out_2(7)
            up(5)
            turn_n3(2)
            up(6)
            feed_down(0)
            up(7)
            feed_down(1)
            up(8)
            turn_n3(3)
            up(9)
            feed_down(2)
            up(10)
            up(11)
            feed_down(3)
            up(12)
            turn_tgt(0)
            up(13)
            feed_down(4)
            up(14)
            up(15)
            turn_tgt(1)
            feed_down(5)
            expert_up(0)
            expert_up(1)
            feed_down(6)
            expert_up(2)
            expert_up(3)
            feed_down(7)
            expert_up(4)
            turn_tgt(2)
            expert_up(5)
            expert_down(0)
            expert_up(6)
            expert_up(7)
            expert_down(1)
            expert_up(8)
            turn_tgt(3)
            expert_up(9)
            expert_down(2)
            expert_up(10)
            expert_up(11)
            expert_down(3)
            expert_up(12)
            expert_up(13)
            expert_down(4)
            expert_up(14)
            expert_up(15)
            for k in range(5, 8):
                expert_down(k)


_X = "L0_xcond_"
_AS_IS = (["x"] + [_X + v for v in ("attn1_wv", "attn1_wo", "attn1_bo", "attn2_wk", "attn2_wv", "attn2_wo", "attn2_bo",
                                    "ff_w1", "ff_w2", "ff_b2", "norm1_w", "norm2_w", "norm3_w")]
          + ["L0_ffn_" + v for v in ("w1", "w2", "b2", "gamma", "beta")])


def kernel(**inputs):
    import numpy as _np
    import concourse.bacc as _bacc
    from concourse import mybir as _mybir
    from concourse.bass_utils import run_bass_kernel_spmd as _run

    nc = _bacc.Bacc("TRN2", target_bir_lowering=False, num_devices=1)
    laid = {name: _np.asarray(inputs[name]) for name in _AS_IS}
    laid["wq1T"] = _np.asarray(inputs[_X + "attn1_wq"]).T
    laid["wk1T"] = _np.asarray(inputs[_X + "attn1_wk"]).T
    laid["wq2T"] = _np.asarray(inputs[_X + "attn2_wq"]).T
    laid["ctxT"] = _np.asarray(inputs["ctx_1024"]).reshape(B * CTX, D).T
    laid["cols"] = _np.concatenate([_np.asarray(v).reshape(-1, P) for v in (
        inputs["cond_1024"], inputs[_X + "norm1_b"], inputs[_X + "norm2_b"], inputs[_X + "norm3_b"], inputs[_X + "ff_b1"],
        inputs["L0_ffn_b1"][0])]).T
    arrays, args = {}, {}
    for name, v in laid.items():
        v = _np.ascontiguousarray(v)
        arrays[f"in_{name}"] = v
        args[name] = nc.dram_tensor(f"in_{name}", v.shape, _mybir.dt.from_np(v.dtype), kind="ExternalInput").ap()
    out = nc.dram_tensor("out_0", (B, S, D), F32, kind="ExternalOutput").ap()
    residual_block(nc, args, out)
    r = _run(nc, [arrays], core_ids=[0])
    return r.results[0]["out_0"]
```
